# Optimizing a Trainium2 kernel written in Bass

```python
import numpy as np
import jax
import jax.numpy as jnp

def _softmax(x, axis=-1):
    return jax.nn.softmax(x, axis=axis)

def _gelu(x):
    return jax.nn.gelu(x, approximate=True)

def _silu(x):
    return jax.nn.silu(x)

def _sigmoid(x):
    return jax.nn.sigmoid(x)

def _layernorm(x, axis=-1, eps=1e-05):
    m = jnp.mean(x, axis=axis, keepdims=True)
    v = jnp.var(x, axis=axis, keepdims=True)
    return (x - m) / jnp.sqrt(v + eps)

def _scatter_add(tgt, idx, src, axis=0):
    return tgt.at[idx].add(src)

def _segment_sum(src, seg, n):
    return jax.ops.segment_sum(src, seg, n)
kernel_name = 'mk_xattn_ffn_d1_seqx_r8_2a81ad'

def setup_inputs(seed: int=0):
    np.random.seed(seed)
    _w = jnp.asarray

    def _rec_inputs():
        import jax
        import jax.numpy as jnp
        _rk = jax.random.key(seed)
        x = -0.0003929 + 0.9999 * jax.random.normal(jax.random.fold_in(_rk, 1), (128, 64, 128), jnp.float32)
        _lenS = 64 - jax.random.randint(jax.random.fold_in(_rk, 7), (128,), 0, max(1, 64 // 4) + 1, jnp.int32)
        _lenS2 = 64 - jax.random.randint(jax.random.fold_in(_rk, 8), (128,), 0, max(1, 64 // 4) + 1, jnp.int32)
        _ctx_1024P = jax.random.normal(jax.random.fold_in(_rk, 11), (128, 16, 128), jnp.float32)
        _ctx_1024c = jax.random.dirichlet(jax.random.fold_in(_rk, 511), 0.3 * jnp.ones((16,), jnp.float32), (128, 64))
        _ctx_1024t = jnp.einsum('bsk,bkd->bsd', _ctx_1024c, _ctx_1024P)
        _ctx_1024t = _ctx_1024t * jax.lax.rsqrt(jnp.mean(jnp.square(_ctx_1024t)) + 1e-12) * 0.953939
        ctx_1024 = 2.81802e-05 + 1.00001 * (_ctx_1024t + 0.3 * jax.random.normal(jax.random.fold_in(_rk, 611), (128, 64, 128), jnp.float32))
        return (x, ctx_1024)
    x, ctx_1024 = _rec_inputs()

    def _L0_xattn_setup():
        import jax, jax.numpy as jnp
        import numpy as np
        NUM_HEADS = 16
        EPS = 1e-12

        def _l2_normalize(x):
            n = jnp.sqrt(jnp.sum(x * x, axis=-1, keepdims=True))
            return x / jnp.maximum(n, EPS)
        key = jax.random.key(seed)
        ks = jax.random.split(key, 9)
        B, L, S, D = (4, 512, 512, 128)
        s = 1.0 / np.sqrt(D)
        return {'q': jax.random.normal(ks[0], (B, L, D), jnp.float32), 'k': jax.random.normal(ks[1], (B, S, D), jnp.float32), 'v': jax.random.normal(ks[2], (B, S, D), jnp.float32), 'Wq': jax.random.normal(ks[3], (D, D), jnp.float32) * s, 'bq': jax.random.normal(ks[4], (D,), jnp.float32) * 0.01, 'Wk': jax.random.normal(ks[5], (D, D), jnp.float32) * s, 'bk': jax.random.normal(ks[6], (D,), jnp.float32) * 0.01, 'Wv': jax.random.normal(ks[7], (D, D), jnp.float32) * s, 'bv': jax.random.normal(ks[8], (D,), jnp.float32) * 0.01}
    _L0_xattn_all = _L0_xattn_setup()
    _L0_xattn_in = {k: v for k, v in _L0_xattn_all.items() if k in ('Wq', 'bq', 'Wk', 'bk', 'Wv', 'bv')}
    del _L0_xattn_all

    def _L0_ffn_setup():
        import jax, jax.numpy as jnp
        import numpy as np
        import math
        B, S, H, I, E = (4, 256, 128, 512, 8)
        TOP_K = 2
        CAPACITY_FACTOR = 1.25
        key = jax.random.key(seed)
        k1, k2, k3, k4, k5 = jax.random.split(key, 5)
        x = jax.random.normal(k1, (B, S, H), dtype=jnp.float32)
        W_router = jax.random.normal(k2, (E, H), dtype=jnp.float32) * (1.0 / math.sqrt(H))
        b_router = jnp.zeros((E,), dtype=jnp.float32)
        experts_inter = jax.random.normal(k3, (E, H, I), dtype=jnp.float32) * 0.02
        experts_out = jax.random.normal(k4, (E, I, H), dtype=jnp.float32) * 0.02
        return {'x': x, 'W_router': W_router, 'b_router': b_router, 'experts_inter': experts_inter, 'experts_out': experts_out}
    _L0_ffn_all = _L0_ffn_setup()
    _L0_ffn_in = {k: v for k, v in _L0_ffn_all.items() if k in ('W_router', 'b_router', 'experts_inter', 'experts_out')}
    del _L0_ffn_all
    return {'x': x, 'ctx_1024': ctx_1024, 'L0_xattn_Wq': _L0_xattn_in['Wq'], 'L0_xattn_bq': _L0_xattn_in['bq'], 'L0_xattn_Wk': _L0_xattn_in['Wk'], 'L0_xattn_bk': _L0_xattn_in['bk'], 'L0_xattn_Wv': _L0_xattn_in['Wv'], 'L0_xattn_bv': _L0_xattn_in['bv'], 'L0_ffn_W_router': _L0_ffn_in['W_router'], 'L0_ffn_b_router': _L0_ffn_in['b_router'], 'L0_ffn_experts_inter': _L0_ffn_in['experts_inter'], 'L0_ffn_experts_out': _L0_ffn_in['experts_out']}

def reference(x, ctx_1024, L0_xattn_Wq, L0_xattn_bq, L0_xattn_Wk, L0_xattn_bk, L0_xattn_Wv, L0_xattn_bv, L0_ffn_W_router, L0_ffn_b_router, L0_ffn_experts_inter, L0_ffn_experts_out):
    import jax
    import jax.numpy as jnp

    def _L0_xattn_ref(q, k, v, Wq, bq, Wk, bk, Wv, bv):
        import jax, jax.numpy as jnp
        import numpy as np
        NUM_HEADS = 16
        EPS = 1e-12

        def _l2_normalize(x):
            n = jnp.sqrt(jnp.sum(x * x, axis=-1, keepdims=True))
            return x / jnp.maximum(n, EPS)
        B = q.shape[0]
        H = NUM_HEADS
        qp = q @ Wq.T + bq
        kp = k @ Wk.T + bk
        vp = v @ Wv.T + bv

        def split(x):
            Bx, T, D = x.shape
            return x.reshape(Bx, T, H, D // H).transpose(0, 2, 1, 3)
        qh = split(qp)
        kh = _l2_normalize(split(kp))
        vh = _l2_normalize(split(vp))
        kv = jnp.einsum('bhsi,bhsj->bhij', kh, vh)
        xh = jnp.einsum('bhli,bhij->bhlj', qh, kv)
        Bx, Hh, L, I = xh.shape
        return xh.transpose(0, 2, 1, 3).reshape(Bx, L, Hh * I)

    def _L0_ffn_ref(x, W_router, b_router, experts_inter, experts_out):
        import jax, jax.numpy as jnp
        import numpy as np
        import math
        B, S, H, I, E = (4, 256, 128, 512, 8)
        TOP_K = 2
        CAPACITY_FACTOR = 1.25
        b, s, h = x.shape
        e = experts_inter.shape[0]
        T = b * s
        capacity = math.ceil(T / e * CAPACITY_FACTOR)
        x_flat = x.reshape(T, h)
        logits = x_flat @ W_router.T + b_router
        weights_flat = jax.nn.softmax(logits, axis=-1)
        top_vals, top_idx = jax.lax.top_k(weights_flat, TOP_K)
        topk_flat = jnp.zeros_like(weights_flat).at[jnp.arange(T)[:, None], top_idx].set(top_vals)
        routing_mask = (topk_flat > 0).astype(jnp.int32)
        order = jnp.argsort(-routing_mask, axis=0, stable=True)
        sorted_mask = jnp.take_along_axis(routing_mask, order, axis=0)
        sorted_mask = sorted_mask[:capacity]
        sorted_idx = order[:capacity]
        used_tokens = (sorted_idx * sorted_mask).reshape(-1)
        mask_flat = sorted_mask.reshape(-1).astype(x.dtype)
        inputs_tokens = x_flat[used_tokens] * mask_flat[:, None]
        inputs_tokens = inputs_tokens.reshape(capacity, e, h)
        inputs_weights = jnp.take_along_axis(topk_flat, sorted_idx, axis=0)
        hmid = jnp.einsum('ceh,ehi->cei', inputs_tokens, experts_inter)
        hmid = jax.nn.relu(hmid)
        out = jnp.einsum('cei,eih->ceh', hmid, experts_out)
        out = out * inputs_weights[:, :, None]
        combined = jnp.zeros((T, h), dtype=x.dtype).at[used_tokens].add(out.reshape(-1, h))
        return combined.reshape(b, s, h)
    x = x + _L0_xattn_ref(_layernorm(x, axis=-1), ctx_1024, ctx_1024, L0_xattn_Wq, L0_xattn_bq, L0_xattn_Wk, L0_xattn_bk, L0_xattn_Wv, L0_xattn_bv)
    x = x + _L0_ffn_ref(_layernorm(x, axis=-1), L0_ffn_W_router, L0_ffn_b_router, L0_ffn_experts_inter, L0_ffn_experts_out)
    return x

_drawn_inputs = setup_inputs


def setup_inputs(seed=0):
    import zlib

    import numpy as np

    out = dict(_drawn_inputs(seed))
    spreads = {'L0_ffn_b_router': (0.0, 0.8)}
    factors = {'L0_xattn_bq': 5.568,
     'L0_xattn_bk': 3.337,
     'L0_xattn_bv': 3.334,
     'L0_ffn_W_router': 8.0,
     'L0_ffn_experts_inter': 8.0,
     'L0_ffn_experts_out': 8.0}
    for name, (base, spread) in spreads.items():
        noise = np.random.default_rng([zlib.crc32(name.encode()), seed]).standard_normal(out[name].shape)
        drawn = base * np.exp(spread * noise) if base else spread * noise
        out[name] = jnp.asarray(drawn.astype(out[name].dtype))
    for name, factor in factors.items():
        out[name] = (out[name] * factor).astype(out[name].dtype)
    return out
```

```python
import concourse.bass as bass
from concourse import mybir
from contextlib import ExitStack

F32 = mybir.dt.float32
BF16 = mybir.dt.bfloat16
I32 = mybir.dt.int32
U32 = mybir.dt.uint32
ALU = mybir.AluOpType
ACT = mybir.ActivationFunctionType
AX = mybir.AxisListType

P = 128
BATCHES, SEQ, D = 128, 64, 128
HEADS, HD = 16, 8
EXPERTS, INNER, TOP_K = 8, 512, 2
TOKENS = BATCHES * SEQ
CAPACITY = -(-TOKENS * 5 // (EXPERTS * 4))
TILES = TOKENS // P
G = 4
CHUNKS = TILES // G
TOK = G * P
SLOTS = EXPERTS * CAPACITY
SLOT_TILES = CAPACITY // P
ROW_GATE, ROW_TOKEN, ROW = D, D + EXPERTS, D + EXPERTS + 1
NO_SLOT = 16384.0
LN_EPS, L2_EPS = 1e-5, 1e-12
HEAD = 4
RING = 4
IT = INNER // P
DVE_PER_STEP = 23
PAIR = 2
GROUPS = SLOT_TILES // PAIR
PG = PAIR * P
GROUP_HEAD = 2


class Chunk:

    def __init__(self, it, k):
        self.it, self.k = it, k

    def back(self, n):
        k = self.k - n
        return Chunk(self.it + (k // RING), k % RING)

    @property
    def number(self):
        return self.it * RING + self.k

    @property
    def known(self):
        return isinstance(self.it, int)

    def valid(self):
        return not self.known or 0 <= self.number < CHUNKS


def done(chunk):
    return chunk.number + (1 + HEAD)


class Group:

    def __init__(self, i, j):
        self.i, self.j = i + j // (2 * GROUPS), j % (2 * GROUPS)
        self.par, self.g = self.j // GROUPS, self.j % GROUPS
        self.b = self.j % 2
        self.expert = self.i * 2 + self.par

    def next(self, n):
        return Group(self.i, self.j + n)

    def valid(self):
        return not isinstance(self.i, int) or 0 <= self.i < EXPERTS // 2


def group_done(group):
    return group.i * (2 * GROUPS) + (group.j + 1 + GROUP_HEAD)


def group_steps(step):
    def run(engine):
        turns = EXPERTS // 2 - 1
        step(Group(0, -1))
        step(Group(0, 0))
        with engine.Fori(0, turns) as i:
            for j in range(1, 2 * GROUPS + 1):
                step(Group(i, j))
        for j in range(1, 2 * GROUPS + 1):
            step(Group(turns, j))
    return run


class Local:

    def __init__(self, engine, sem):
        self.engine, self.sem, self.count, self.base = engine, sem, 0, 0

    def add(self, instruction):
        instruction.then_inc(self.sem, 1)
        self.count += 1

    def wait(self, apart=None):
        self.engine.wait_ge(self.sem, self.base + self.count)
        if apart is not None:
            self.engine.sem_inc(apart, 1)


def steps(engine, step, local=None, per_step=0):
    first, last = RING - 1, CHUNKS - 1
    for s in range(-1, first):
        step(Chunk(s // RING, s % RING))
    start = local.count if local else 0
    turns = (last - first) // RING
    with engine.Fori(1, 1 + turns) as i:
        if local:
            local.base, local.count = (i - 1) * (RING * per_step), start
        for k in range(RING):
            step(Chunk(i, k).back(1))
        if local:
            assert local.count - start == RING * per_step, (local.count - start, per_step)
    if local:
        local.base, local.count = 0, start + turns * RING * per_step
    for s in range(last, CHUNKS + 3):
        step(Chunk(s // RING, s % RING))


def build(nc, x, ctx_t, wq_t, bq, wkv_t, bkv, wr_t, br, w_in, w_out, out, slots):
    with ExitStack() as stack:
        def sb(name, shape, dt=F32):
            return stack.enter_context(nc.sbuf_tensor(name, shape, dt))

        def sem(name):
            return stack.enter_context(nc.semaphore(name))

        wq_sb = sb("wq_sb", [P, D])
        wkv_sb = sb("wkv_sb", [P, 2 * D])
        wr_sb = sb("wr_sb", [P, EXPERTS])
        bq_sb = sb("bq_sb", [P, 1])
        bkv_sb = sb("bkv_sb", [P, 2 * D])
        br_sb = sb("br_sb", [P, EXPERTS])
        eps_sb = sb("eps_sb", [P, 1])
        ident = sb("ident", [P, P])
        head_mask = sb("head_mask", [P, D])
        before = sb("before", [P, P], BF16)
        ones = sb("ones", [P, P], BF16)
        iota8 = sb("iota8", [P, EXPERTS])
        slot_base = sb("slot_base", [P, EXPERTS])
        token_no = sb("token_no", [P, TILES], I32)
        empty_row = sb("empty_row", [P, ROW])
        x_sb = sb("x_sb", [P, RING, G, D])
        ct_sb = sb("ct_sb", [P, RING, TOK])
        rows = sb("rows", [P, RING, G, ROW])
        xn = sb("xn", [P, 2, G, D])
        xnt = sb("xnt", [P, TOK])
        qt = sb("qt", [P, 2, TOK])
        kvb = sb("kvb", [P, 2, G, 2, D])
        sq = sb("sq", [P, G, 2, D])
        ss = sb("ss", [P, G, 2, HEADS])
        kv_norm = sb("kv_norm", [P, G, 2, HEADS])
        key_scale = sb("key_scale", [P, G, HEADS])
        state = sb("state", [P, 2, G, D])
        x1 = sb("x1", [P, 2, G, D])
        x2t = sb("x2t", [P, TOK])
        st1 = sb("st1", [P, 2, G, 6])
        mv1 = sb("mv1", [P, 2, G, 2])
        sd1 = sb("sd1", [P, G])
        sc1 = sb("sc1", [P, 2, 2, G])
        st2 = sb("st2", [P, 2, G, 6])
        mv2 = sb("mv2", [P, 2, G, 2])
        sd2 = sb("sd2", [P, G])
        sc2 = sb("sc2", [P, 2, 2, G])
        logit = sb("logit", [P, G, EXPERTS])
        best = sb("best", [P, G, 8])
        best_no = sb("best_no", [P, G, 8], U32)
        shifted = sb("shifted", [P, G, EXPERTS])
        expo = sb("expo", [P, G, EXPERTS])
        total = sb("total", [P, G])
        prob = sb("prob", [P, G, EXPERTS])
        chosen = sb("chosen", [P, G, TOP_K, EXPERTS])
        either = sb("either", [P, G, EXPERTS])
        routed = sb("routed", [P, G, EXPERTS], BF16)
        in_chunk = sb("in_chunk", [P, EXPERTS])
        earlier = sb("earlier", [P, 2, EXPERTS], BF16)
        fits = sb("fits", [P, G, EXPERTS])
        place = sb("place", [P, G, EXPERTS])
        place_k = sb("place_k", [P, G, TOP_K, EXPERTS])
        place_f = sb("place_f", [P, G, TOP_K])
        place_no = sb("place_no", [P, RING, G * TOP_K], I32)
        wi_sb = sb("wi_sb", [P, 2, INNER])
        wo_sb = sb("wo_sb", [P, 2, IT, D])
        xg = sb("xg", [P, 2, SLOT_TILES, ROW])
        gate = sb("gate", [P, 2, SLOT_TILES])
        xgt = sb("xgt", [P, 2, PG])
        hid = sb("hid", [P, 2, IT, PG])
        y_sb = sb("y_sb", [P, 2, SLOT_TILES, D])

        ps0, ps1, ps2, ps3 = [stack.enter_context(nc.psum_tensor(f"ps{i}", [P, 1024], F32)) for i in range(4)]
        ps_kv = ps0[:, :].rearrange("p (g a d) -> p g a d", g=G, a=2)
        ps_state = ps1[:, :].rearrange("p (h g d) -> p h g d", h=2, g=G)
        ps_t, ps_q = ps2[:, 0:512], ps2[:, 512:1024]
        ps_o = ps3[:, 0:512].rearrange("p (g d) -> p g d", g=G)
        ps_logit = ps3[:, 512:512 + G * EXPERTS].rearrange("p (g e) -> p g e", g=G)
        ps_rank = ps3[:, 768:768 + G * EXPERTS].rearrange("p (g e) -> p g e", g=G)

        small_loaded = sem("small_loaded")
        consts_made = sem("consts_made")
        x_loaded = [sem(f"x_loaded{b}") for b in range(RING)]
        ct_loaded = [sem(f"ct_loaded{b}") for b in range(RING)]
        rows_sent = [sem(f"rows_sent{b}") for b in range(RING)]
        x1_stored = [sem(f"x1_stored{b}") for b in range(2)]
        dummies_stored = sem("dummies_stored")
        ln1_scaled, x_normed, x_turned, xnt_made = map(sem, ("ln1_scaled", "x_normed", "x_turned", "xnt_made"))
        kv_projected, q_projected, qt_made = map(sem, ("kv_projected", "q_projected", "qt_made"))
        kv_biased, kv_squared, kv_rooted, norms_ready, kn_made = map(
            sem, ("kv_biased", "kv_squared", "kv_rooted", "norms_ready", "kn_made"))
        state_summed, state_made, attended, x1_made = map(
            sem, ("state_summed", "state_made", "attended", "x1_made"))
        ln1_var, ln1_root, ln2_var, ln2_root, ln2_scaled = map(
            sem, ("ln1_var", "ln1_root", "ln2_var", "ln2_root", "ln2_scaled"))
        rows_normed, rows_turned, x2t_made, logits_ready = map(
            sem, ("rows_normed", "rows_turned", "x2t_made", "logits_ready"))
        shift_ready, exp_ready, routed_ready, rank_ready, place_ready = map(
            sem, ("shift_ready", "exp_ready", "routed_ready", "rank_ready", "place_ready"))
        dve_order = sem("dve_order")
        pool_order = sem("pool_order")
        waits_apart = sem("waits_apart")
        weights_loaded = [sem(f"weights_loaded{b}") for b in range(2)]
        xg_loaded = [sem(f"xg_loaded{b}") for b in range(2)]
        group_turned, xgt_made, up_done, hid_act, hid_dve = map(
            sem, ("group_turned", "xgt_made", "up_done", "hid_act", "hid_dve"))
        down_done, y_made, rows_added, experts_added, gates_made = map(
            sem, ("down_done", "y_made", "rows_added", "experts_added", "gates_made"))

        x_c = x.rearrange("(c g p) d -> c p g d", g=G, p=P)
        out_c = out[0:TOKENS, :].rearrange("(c g p) d -> c p g d", g=G, p=P)
        slots_e = slots.rearrange("(e j p) r -> e p j r", e=EXPERTS, p=P)

        def head_start(engine, *sems):
            for s in sems:
                engine.sem_inc(s, HEAD)

        def group_head_start(engine, *sems):
            for s in sems:
                engine.sem_inc(s, GROUP_HEAD)

        block = stack.enter_context(nc.Block())

        @block.sync
        def _(sp):
            def load(c):
                if not c.valid():
                    return
                if not (c.known and c.number < RING):
                    sp.wait_ge(x1_made, done(c.back(RING)))
                    sp.wait_ge(kv_projected, done(c.back(RING)))
                if c.known:
                    x_src, ct_src = x_c[c.number], ctx_t[:, c.number * TOK:(c.number + 1) * TOK]
                else:
                    x_src = x_c[bass.ds(c.number, 1)].rearrange("c p g d -> (c p) g d")
                    ct_src = ctx_t[:, bass.ds(c.number * TOK, TOK)]
                sp.dma_start(x_sb[:, c.k], x_src).then_inc(x_loaded[c.k], 16)
                sp.dma_start(ct_sb[:, c.k, :], ct_src).then_inc(ct_loaded[c.k], 16)

            def store(c):
                if not c.valid():
                    return
                sp.wait_ge(x1_made, done(c))
                dst = out_c[c.number] if c.known else \
                    out_c[bass.ds(c.number, 1)].rearrange("c p g d -> (c p) g d")
                sp.dma_start(dst, x1[:, c.k % 2]).then_inc(x1_stored[c.k % 2], 16)

            def step(s):
                load(s.back(-1))
                store(s.back(1))
                if s.known and s.number == -1:
                    sp.wait_ge(consts_made, 2)
                    sp.dma_start(out[TOKENS:TOKENS + P, :], empty_row[:, 0:D]).then_inc(dummies_stored, 16)
                    for par in range(2):
                        load_weights(0, par)

            def load_weights(i, par):
                e = i * 2 + par
                if isinstance(e, int):
                    up, down = w_in[e], w_out[e]
                else:
                    up = w_in[bass.ds(e, 1)].rearrange("e h i -> (e h) i")
                    down = w_out[bass.ds(e, 1)].rearrange("e i h -> (e i) h")
                sp.dma_start(wi_sb[:, par, :], up).then_inc(weights_loaded[par], 16)
                sp.dma_start(wo_sb[:, par], down.rearrange("(t p) h -> p t h", p=P)).then_inc(weights_loaded[par], 16)

            def load_slots(i, par):
                e = i * 2 + par
                src = slots_e[e] if isinstance(e, int) else \
                    slots_e[bass.ds(e, 1)].rearrange("e p j r -> (e p) j r")
                sp.dma_start(xg[:, par], src).then_inc(xg_loaded[par], 16)

            sp.dma_start(wq_sb[:, :], wq_t).then_inc(small_loaded, 16)
            sp.dma_start(wkv_sb[:, :], wkv_t).then_inc(small_loaded, 16)
            sp.dma_start(wr_sb[:, :], wr_t).then_inc(small_loaded, 16)
            sp.dma_start(bq_sb[:, :], bq.rearrange("(p a) -> p a", a=1)).then_inc(small_loaded, 16)
            sp.dma_start(bkv_sb[:, :], bkv.rearrange("(a d) -> a d", a=1).broadcast_to([P, 2 * D])).then_inc(small_loaded, 16)
            sp.dma_start(br_sb[:, :], br.rearrange("(a d) -> a d", a=1).broadcast_to([P, EXPERTS])).then_inc(small_loaded, 16)
            steps(sp, step)
            for b in range(RING):
                sp.wait_ge(rows_sent[b], G * TOP_K * 16 * (CHUNKS // RING + 1))
            for par in range(2):
                load_slots(0, par)
            with sp.Fori(1, EXPERTS // 2) as i:
                for par in range(2):
                    sp.wait_ge(experts_added, i * 2 + (par + 1))
                    load_slots(i, par)
                    load_weights(i, par)

        @block.gpsimd
        def _(pool):
            order = Local(pool, pool_order)
            order.add(pool.memset(empty_row[:, :], 0.0))
            order.add(pool.memset(ident[:, :], 0.0))
            order.add(pool.memset(head_mask[:, :], 1.0))
            order.add(pool.memset(before[:, :], 1.0))
            pool.memset(ones[:, :], 1.0)
            pool.memset(eps_sb[:, :], LN_EPS)
            order.wait()
            order.add(pool.affine_select(out=ident[:, :], in_=ident[:, :], compare_op=ALU.not_equal, fill=1.0,
                                         base=0, pattern=[[-1, P]], channel_multiplier=1))
            order.add(pool.affine_select(out=head_mask[:, :], in_=head_mask[:, :], compare_op=ALU.is_ge, fill=0.0,
                                         base=0, pattern=[[-HD, HEADS], [0, HD]], channel_multiplier=1))
            order.wait()
            pool.affine_select(out=head_mask[:, :], in_=head_mask[:, :], compare_op=ALU.is_ge, fill=0.0,
                               base=HD - 1, pattern=[[HD, HEADS], [0, HD]], channel_multiplier=-1)
            pool.affine_select(out=before[:, :], in_=before[:, :], compare_op=ALU.is_gt, fill=0.0,
                               base=0, pattern=[[1, P]], channel_multiplier=-1)
            pool.iota(iota8[:, :], pattern=[[1, EXPERTS]], base=0, channel_multiplier=0,
                      allow_small_or_imprecise_dtypes=True)
            pool.iota(slot_base[:, :], pattern=[[CAPACITY, EXPERTS]], base=-int(NO_SLOT), channel_multiplier=0,
                      allow_small_or_imprecise_dtypes=True)
            pool.iota(token_no[:, :], pattern=[[P, TILES]], base=0, channel_multiplier=1)
            pool.iota(empty_row[:, ROW_TOKEN:ROW].bitcast(I32), pattern=[[0, 1]], base=TOKENS,
                      channel_multiplier=1).then_inc(pool_order, 1)
            order.count += 1
            order.wait()
            pool.drain().then_inc(consts_made, 2)
            pool.sem_inc(experts_added, 2)
            per = EXPERTS // RING
            for e in range(EXPERTS):
                pool.dma_start(slots_e[e], empty_row[:, None, :].broadcast_to([P, SLOT_TILES, ROW])) \
                    .then_inc(rows_sent[e // per], G * TOP_K * 16 // per)

            def step(s):
                c = s.back(3)
                if not c.valid():
                    return
                pool.wait_ge(place_ready, done(c))
                pool.sem_inc(waits_apart, 1)
                for g in range(G):
                    for k in range(TOP_K):
                        j = g * TOP_K + k
                        pool.indirect_dma_start(
                            slots[:, :], bass.IndirectOffsetOnAxis(
                                ap=place_no[:, c.k, j:j + 1], axis=0),
                            rows[:, c.k, g, :], None, bounds_check=SLOTS - 1, oob_is_err=False,
                        ).then_inc(rows_sent[c.k], 16)

            for b in range(RING):
                pool.wait_ge(rows_sent[b], G * TOP_K * 16)
            steps(pool, step)

            for b in range(2):
                pool.wait_ge(x1_stored[b], 16 * (CHUNKS // 2))
            pool.wait_ge(dummies_stored, 16)
            with pool.Fori(0, EXPERTS // 2) as i:
                for par in range(2):
                    e = i * 2 + par
                    for g in range(GROUPS):
                        pool.wait_ge(y_made, group_done(Group(i, par * GROUPS + g)))
                        pool.sem_inc(waits_apart, 1)
                        for t in range(PAIR):
                            j = g * PAIR + t
                            pool.indirect_dma_start(
                                out[:, :], bass.IndirectOffsetOnAxis(
                                    ap=xg[:, par, j, ROW_TOKEN:ROW].bitcast(I32), axis=0),
                                y_sb[:, par, j, :], None, compute_op=ALU.add,
                            ).then_inc(rows_added, 16)
                    pool.wait_ge(rows_added, e * (16 * SLOT_TILES) + 16 * SLOT_TILES)
                    pool.sem_inc(experts_added, 1)

        @block.scalar
        def _(act):
            head_start(act, ln1_root, ln2_root, x_normed, xnt_made, qt_made, kv_squared, kv_rooted, rows_normed,
                       x2t_made, exp_ready)
            act.wait_ge(consts_made, 2)
            act.wait_ge(small_loaded, 16 * 6)

            def root1(c):
                if not c.valid():
                    return
                act.wait_ge(ln1_var, done(c))
                if not (c.known and c.number < 1):
                    act.wait_ge(ln1_scaled, done(c.back(1)))
                act.activation(sd1[:, :], mv1[:, c.k % 2, :, 1], ACT.Sqrt, bias=eps_sb[:, :]).then_inc(ln1_root, 1)

            def norm1(c):
                if not c.valid():
                    return
                act.wait_ge(ln1_scaled, done(c))
                if not (c.known and c.number < 2):
                    act.wait_ge(x_turned, done(c.back(2)))
                for g in range(G):
                    ins = act.activation(xn[:, c.k % 2, g, :], x_sb[:, c.k, g, :], ACT.Identity,
                                         scale=sc1[:, c.k % 2, 0, g:g + 1], bias=sc1[:, c.k % 2, 1, g:g + 1])
                ins.then_inc(x_normed, 1)

            def step(s):
                c = s
                if c.valid():
                    act.wait_ge(x_turned, done(c))
                    if not (c.known and c.number < 1):
                        act.wait_ge(q_projected, done(c.back(1)))
                    act.copy(xnt[:, :], ps_t).then_inc(xnt_made, 1)
                c = s.back(3)
                if c.valid():
                    act.wait_ge(shift_ready, done(c))
                    act.activation(expo[:, :, :], shifted[:, :, :], ACT.Exp).then_inc(exp_ready, 1)
                root1(s.back(-1))
                c = s
                if c.valid():
                    act.wait_ge(kv_biased, done(c))
                    act.activation(sq[:, :, :, :], kvb[:, c.k % 2], ACT.Square).then_inc(kv_squared, 1)
                norm1(s.back(-1))
                if c.valid():
                    act.wait_ge(norms_ready, done(c))
                    act.activation(kv_norm[:, :, :, :],
                                   ss[:, :, :, :], ACT.Sqrt).then_inc(kv_rooted, 1)
                    act.wait_ge(q_projected, done(c))
                    if not (c.known and c.number < 2):
                        act.wait_ge(attended, done(c.back(2)))
                    act.activation(qt[:, c.k % 2, :], ps_q, ACT.Identity, bias=bq_sb[:, :]).then_inc(qt_made, 1)
                c = s.back(2)
                if c.valid():
                    act.wait_ge(rows_turned, done(c))
                    if not (c.known and c.number < 1):
                        act.wait_ge(logits_ready, done(c.back(1)))
                    act.copy(x2t[:, :], ps_t).then_inc(x2t_made, 1)
                c = s.back(1)
                if c.valid():
                    act.wait_ge(ln2_var, done(c))
                    if not (c.known and c.number < 1):
                        act.wait_ge(ln2_scaled, done(c.back(1)))
                    act.activation(sd2[:, :], mv2[:, c.k % 2, :, 1], ACT.Sqrt, bias=eps_sb[:, :]).then_inc(ln2_root, 1)
                    act.wait_ge(ln2_scaled, done(c))
                    if not (c.known and c.number < RING):
                        act.wait_ge(rows_sent[c.k], (c.it + 1) * (G * TOP_K * 16))
                    for g in range(G):
                        ins = act.activation(rows[:, c.k, g, 0:D], x1[:, c.k % 2, g, :], ACT.Identity,
                                             scale=sc2[:, c.k % 2, 0, g:g + 1], bias=sc2[:, c.k % 2, 1, g:g + 1])
                    ins.then_inc(rows_normed, 1)

            steps(act, step)

            group_head_start(act, xgt_made, hid_act)

            def b_step(n):
                t = n.next(1)
                if t.valid():
                    act.wait_ge(group_turned, group_done(t))
                    act.wait_ge(up_done, group_done(t.next(-2)))
                    act.copy(xgt[:, t.b, :], ps2[:, 512 * t.b:512 * t.b + PG]).then_inc(xgt_made, 1)
                if n.valid():
                    act.wait_ge(up_done, group_done(n))
                    act.wait_ge(down_done, group_done(n.next(-2)))
                    act.activation(hid[:, n.b, 0:IT // 2, :],
                                   [ps0, ps1][n.b][:, 0:512].rearrange("p (t s) -> p t s", s=PG),
                                   ACT.Relu).then_inc(hid_act, 1)

            group_steps(b_step)(act)

        @block.vector
        def _(dve):
            order = Local(dve, dve_order)
            head_start(dve, ln1_var, ln1_scaled, kv_biased, norms_ready, kn_made, state_made, x1_made,
                       ln2_var, ln2_scaled, shift_ready, routed_ready, place_ready)
            order.add(dve.memset(earlier[:, 0, :], 0.0))
            dve.wait_ge(consts_made, 2)
            dve.wait_ge(small_loaded, 16 * 6)

            def stats(c, src, st, mv, ready):
                for g in range(G):
                    ins = dve.bn_stats(st[:, c.k % 2, g, :], src[:, g, :])
                order.add(ins)
                order.wait(waits_apart)
                for g in range(G):
                    ins = dve.bn_aggr(mv[:, c.k % 2, g, :], st[:, c.k % 2, g, :])
                ins.then_inc(ready, 1)

            def scales(c, sd, mv, sc, root, ready):
                dve.wait_ge(root, done(c))
                order.add(dve.reciprocal(sc[:, c.k % 2, 0, :], sd[:, :]))
                order.wait()
                dve.scalar_tensor_tensor(sc[:, c.k % 2, 1, :], mv[:, c.k % 2, :, 0], -1.0, sc[:, c.k % 2, 0, :],
                                         ALU.mult, ALU.mult).then_inc(ready, 1)

            def step(s):
                r = s.back(3)
                if r.valid():
                    dve.wait_ge(logits_ready, done(r))
                    order.add(dve.tensor_tensor(logit[:, :, :], ps_logit,
                                                br_sb[:, None, :].broadcast_to([P, G, EXPERTS]), ALU.add))
                    order.wait(waits_apart)
                    for g in range(G):
                        ins = dve.max(best[:, g, :], logit[:, g, :])
                    order.add(ins)
                    order.wait(waits_apart)
                    for g in range(G):
                        ins = dve.max_index(best_no[:, g, :], best[:, g, :], logit[:, g, :])
                    order.add(ins)
                    dve.tensor_tensor(shifted[:, :, :], logit[:, :, :],
                                      best[:, :, 0:1].broadcast_to([P, G, EXPERTS]), ALU.subtract).then_inc(shift_ready, 1)
                n = s.back(-1)
                if n.valid():
                    dve.wait_ge(x_loaded[n.k], (n.it + 1) * 16)
                    if not (n.known and n.number < 2):
                        dve.wait_ge(ln1_scaled, done(n.back(2)))
                    stats(n, x_sb[:, n.k], st1, mv1, ln1_var)
                if r.valid():
                    order.wait()
                    order.add(dve.tensor_tensor(
                        chosen[:, :, :, :], best_no[:, :, 0:TOP_K, None].broadcast_to([P, G, TOP_K, EXPERTS]),
                        iota8[:, None, None, :].broadcast_to([P, G, TOP_K, EXPERTS]), ALU.is_equal))
                    tile = r.number * G
                    tiles = token_no[:, tile:tile + G] if r.known else token_no[:, bass.ds(tile, G)]
                    dve.tensor_copy(rows[:, r.k, :, ROW_TOKEN].bitcast(I32), tiles)
                    order.wait()
                    order.add(dve.tensor_tensor(either[:, :, :], chosen[:, :, 0, :], chosen[:, :, 1, :], ALU.add))
                    dve.wait_ge(exp_ready, done(r))
                    order.add(dve.tensor_reduce(total[:, :], expo[:, :, :], AX.X, ALU.add))
                    order.wait()
                    order.add(dve.reciprocal(total[:, :], total[:, :]))
                    order.wait()
                    order.add(dve.tensor_tensor(prob[:, :, :], expo[:, :, :],
                                                total[:, :, None].broadcast_to([P, G, EXPERTS]), ALU.mult))
                    order.wait()
                    order.add(dve.tensor_tensor(rows[:, r.k, :, ROW_GATE:ROW_TOKEN], prob[:, :, :], either[:, :, :],
                                                ALU.mult))
                    order.wait()
                    dve.tensor_scalar(routed[:, :, :], rows[:, r.k, :, ROW_GATE:ROW_TOKEN], 0.0, None,
                                      ALU.is_gt).then_inc(routed_ready, 1)
                if n.valid():
                    scales(n, sd1, mv1, sc1, ln1_root, ln1_scaled)
                if s.valid():
                    dve.wait_ge(kv_projected, done(s))
                    if not (s.known and s.number < 2):
                        dve.wait_ge(state_summed, done(s.back(2)))
                    dve.tensor_tensor(kvb[:, s.k % 2], ps_kv,
                                      bkv_sb[:, :].rearrange("p (a d) -> p a d", a=2)[:, None, :, :]
                                      .broadcast_to([P, G, 2, D]), ALU.add).then_inc(kv_biased, 1)
                if r.valid():
                    dve.wait_ge(routed_ready, done(r))
                    order.add(dve.tensor_reduce(in_chunk[:, :], routed[:, :, :].rearrange("p g e -> p e g"),
                                                AX.X, ALU.add))
                    dve.wait_ge(rank_ready, done(r))
                    order.add(dve.scalar_tensor_tensor(fits[:, :, :], ps_rank, float(CAPACITY), routed[:, :, :],
                                                       ALU.is_lt, ALU.mult))
                    order.add(dve.tensor_tensor(place[:, :, :], ps_rank,
                                                slot_base[:, None, :].broadcast_to([P, G, EXPERTS]), ALU.add))
                    order.wait()
                    order.add(dve.tensor_tensor(earlier[:, (r.k + 1) % 2, :], earlier[:, r.k % 2, :], in_chunk[:, :],
                                                ALU.add))
                    order.add(dve.tensor_tensor(place[:, :, :], place[:, :, :], fits[:, :, :], ALU.mult))
                    order.wait()
                    order.add(dve.tensor_tensor(
                        place_k[:, :, :, :], chosen[:, :, :, :],
                        place[:, :, None, :].broadcast_to([P, G, TOP_K, EXPERTS]), ALU.mult))
                    order.wait()
                    order.add(dve.tensor_reduce(place_f[:, :, :], place_k[:, :, :, :], AX.X, ALU.add))
                    order.wait()
                    dve.tensor_scalar(place_no[:, r.k, :], place_f[:, :, :].rearrange("p g k -> p (g k)"),
                                      NO_SLOT, None, ALU.add).then_inc(place_ready, 1)
                a = s.back(1)
                if a.valid():
                    dve.wait_ge(state_summed, done(a))
                    if not (a.known and a.number < 1):
                        dve.wait_ge(attended, done(a.back(1)))
                    dve.tensor_tensor(state[:, :, :, :].rearrange("p h g d -> p (h g) d"),
                                      ps_state.rearrange("p h g d -> p (h g) d"),
                                      head_mask[:, None, :].broadcast_to([P, 2 * G, D]),
                                      ALU.mult).then_inc(state_made, 1)
                if s.valid():
                    dve.wait_ge(kv_squared, done(s))
                    order.add(dve.tensor_reduce(ss[:, :, :, :], sq[:, :, :, :].rearrange("p g a (h i) -> p g a h i", i=HD),
                                                AX.X, ALU.add))
                    order.wait()
                    dve.tensor_scalar(ss[:, :, :, :], ss[:, :, :, :], L2_EPS * L2_EPS, None,
                                      ALU.max).then_inc(norms_ready, 1)
                    dve.wait_ge(kv_rooted, done(s))
                    order.add(dve.tensor_tensor(key_scale[:, :, :], kv_norm[:, :, 0, :], kv_norm[:, :, 1, :], ALU.mult))
                    order.wait()
                    order.add(dve.reciprocal(key_scale[:, :, :], key_scale[:, :, :]))
                    order.wait()
                    for g in range(G):
                        keys = kvb[:, s.k % 2, g, 0, :].rearrange("p (h i) -> p h i", i=HD)
                        ins = dve.tensor_tensor(keys, keys, key_scale[:, g, :, None].broadcast_to([P, HEADS, HD]),
                                                ALU.mult)
                    ins.then_inc(kn_made, 1)
                if a.valid():
                    dve.wait_ge(attended, done(a))
                    if not (a.known and a.number < 2):
                        dve.wait_ge(x1_stored[a.k % 2], (a.it * RING + a.k - a.k % 2) * 8)
                        dve.wait_ge(rows_normed, done(a.back(2)))
                    dve.tensor_tensor(x1[:, a.k % 2], x_sb[:, a.k], ps_o, ALU.add).then_inc(x1_made, 1)
                    dve.wait_ge(x1_made, done(a))
                    stats(a, x1[:, a.k % 2], st2, mv2, ln2_var)
                    scales(a, sd2, mv2, sc2, ln2_root, ln2_scaled)

            steps(dve, step, order, DVE_PER_STEP)

            group_head_start(dve, hid_dve, y_made)

            def b_step(n):
                if n.valid():
                    dve.wait_ge(up_done, group_done(n))
                    dve.wait_ge(down_done, group_done(n.next(-2)))
                    dve.tensor_scalar(hid[:, n.b, IT // 2:IT, :],
                                      [ps0, ps1][n.b][:, 512:1024].rearrange("p (t s) -> p t s", s=PG),
                                      0.0, None, ALU.max).then_inc(hid_dve, 1)
                y = n.next(-1)
                if y.valid():
                    if y.g == 0:
                        dve.wait_ge(experts_added, y.expert + 1)
                        dve.wait_ge(xg_loaded[y.par], y.i * 16 + 16)
                        column = ROW_GATE + y.expert
                        src = xg[:, y.par, :, column] if isinstance(column, int) else \
                            xg[:, y.par, :, bass.ds(column, 1)].rearrange("p j a -> p (j a)")
                        dve.tensor_copy(gate[:, y.par, :], src).then_inc(gates_made, 1)
                        dve.wait_ge(gates_made, y.expert + 1)
                    dve.wait_ge(down_done, group_done(y))
                    for t in range(PAIR):
                        j = y.g * PAIR + t
                        ins = dve.tensor_scalar(y_sb[:, y.par, j, :], ps3[:, 512 * y.b + P * t:512 * y.b + P * (t + 1)],
                                                gate[:, y.par, j:j + 1], None, ALU.mult)
                    ins.then_inc(y_made, 1)

            group_steps(b_step)(dve)

        @block.tensor
        def _(pe):
            head_start(pe, x_turned, kv_projected, q_projected, state_summed, attended, rows_turned, logits_ready,
                       rank_ready)
            pe.wait_ge(consts_made, 2)
            pe.wait_ge(small_loaded, 16 * 6)

            def step(s):
                if s.valid():
                    pe.wait_ge(x_normed, done(s))
                    if not (s.known and s.number < 3):
                        pe.wait_ge(x2t_made, done(s.back(3)))
                    for g in range(G):
                        ins = pe.transpose(ps_t[:, P * g:P * (g + 1)], xn[:, s.k % 2, g, :], ident[:, :])
                    ins.then_inc(x_turned, 1)
                    pe.wait_ge(ct_loaded[s.k], (s.it + 1) * 16)
                    if not (s.known and s.number < 1):
                        pe.wait_ge(kv_biased, done(s.back(1)))
                    for g in range(G):
                        ins = pe.matmul(ps0[:, 256 * g:256 * (g + 1)], ct_sb[:, s.k, P * g:P * (g + 1)], wkv_sb[:, :],
                                        start=True, stop=True)
                    ins.then_inc(kv_projected, 1)
                r = s.back(3)
                if r.valid():
                    pe.wait_ge(routed_ready, done(r))
                    pe.matmul(ps_rank, before[:, :], routed[:, :, :], start=True, stop=False)
                    for g in range(1, G):
                        pe.matmul(ps_rank[:, g:G, :], ones[:, :], routed[:, 0:G - g, :], start=False, stop=False)
                    pe.matmul(ps_rank, ones[:, :], earlier[:, r.k % 2, None, :].broadcast_to([P, G, EXPERTS]),
                              start=False, stop=True).then_inc(rank_ready, 1)
                a = s.back(1)
                if a.valid():
                    pe.wait_ge(kn_made, done(a))
                    if not (a.known and a.number < 1):
                        pe.wait_ge(state_made, done(a.back(1)))
                    for g in range(G):
                        for h in range(2):
                            half = slice(SEQ * h, SEQ * (h + 1))
                            ins = pe.matmul(ps_state[:, h, g, :], kvb[half, a.k % 2, g, 0, :], kvb[half, a.k % 2, g, 1, :],
                                            start=True, stop=True)
                    ins.then_inc(state_summed, 1)
                if s.valid():
                    pe.wait_ge(xnt_made, done(s))
                    if not (s.known and s.number < 1):
                        pe.wait_ge(qt_made, done(s.back(1)))
                    pe.matmul(ps_q, wq_sb[:, :], xnt[:, :], start=True, stop=True).then_inc(q_projected, 1)
                l = s.back(2)
                if l.valid():
                    pe.wait_ge(rows_normed, done(l))
                    if not (s.known and not s.valid()):
                        pe.wait_ge(xnt_made, done(s))
                    for g in range(G):
                        ins = pe.transpose(ps_t[:, P * g:P * (g + 1)], rows[:, l.k, g, 0:D], ident[:, :])
                    ins.then_inc(rows_turned, 1)
                if a.valid():
                    pe.wait_ge(qt_made, done(a))
                    pe.wait_ge(state_made, done(a))
                    if not (a.known and a.number < 1):
                        pe.wait_ge(x1_made, done(a.back(1)))
                    for g in range(G):
                        for h in range(2):
                            tokens = slice(P * g + SEQ * h, P * g + SEQ * (h + 1))
                            ins = pe.matmul(ps_o[SEQ * h:SEQ * (h + 1), g, :], qt[:, a.k % 2, tokens], state[:, h, g, :],
                                            start=True, stop=True)
                    ins.then_inc(attended, 1)
                if l.valid():
                    pe.wait_ge(x2t_made, done(l))
                    if not (l.known and l.number < 1):
                        pe.wait_ge(place_ready, done(l.back(1)))
                    for g in range(G):
                        ins = pe.matmul(ps_logit[:, g, :], x2t[:, P * g:P * (g + 1)], wr_sb[:, :], start=True, stop=True)
                    ins.then_inc(logits_ready, 1)

            steps(pe, step)

            group_head_start(pe, group_turned, up_done, down_done)

            def b_step(n):
                if n.valid():
                    if n.g == 0:
                        pe.wait_ge(weights_loaded[n.par], n.i * 32 + 32)
                    pe.wait_ge(xgt_made, group_done(n))
                    pe.wait_ge(hid_act, group_done(n.next(-2)))
                    pe.wait_ge(hid_dve, group_done(n.next(-2)))
                    for t in range(IT):
                        ins = pe.matmul([ps0, ps1][n.b][:, PG * t:PG * (t + 1)], wi_sb[:, n.par, P * t:P * (t + 1)],
                                        xgt[:, n.b, :], start=True, stop=True)
                    ins.then_inc(up_done, 1)
                t = n.next(1)
                if t.valid():
                    if t.g == 0:
                        pe.wait_ge(xg_loaded[t.par], t.i * 16 + 16)
                    pe.wait_ge(xgt_made, group_done(t.next(-2)))
                    for q in range(PAIR):
                        ins = pe.transpose(ps2[:, 512 * t.b + P * q:512 * t.b + P * (q + 1)],
                                           xg[:, t.par, t.g * PAIR + q, 0:D], ident[:, :])
                    ins.then_inc(group_turned, 1)
                m = n.next(-1)
                if m.valid():
                    pe.wait_ge(hid_act, group_done(m))
                    pe.wait_ge(hid_dve, group_done(m))
                    pe.wait_ge(y_made, group_done(m.next(-2)))
                    for q in range(PAIR):
                        for t in range(IT):
                            ins = pe.matmul(ps3[:, 512 * m.b + P * q:512 * m.b + P * (q + 1)],
                                            hid[:, m.b, t, P * q:P * (q + 1)], wo_sb[:, m.par, t, :],
                                            start=(t == 0), stop=(t == IT - 1))
                    ins.then_inc(down_done, 1)

            group_steps(b_step)(pe)


def kernel(x, ctx_1024, L0_xattn_Wq, L0_xattn_bq, L0_xattn_Wk, L0_xattn_bk, L0_xattn_Wv, L0_xattn_bv,
           L0_ffn_W_router, L0_ffn_b_router, L0_ffn_experts_inter, L0_ffn_experts_out):
    import numpy as np
    import concourse.bacc as bacc
    from concourse.bass_utils import run_bass_kernel_spmd

    nc = bacc.Bacc("TRN2", target_bir_lowering=False, num_devices=1)
    arrays = {
        "x": np.asarray(x).reshape(TOKENS, D),
        "ctx_t": np.asarray(ctx_1024).reshape(TOKENS, D).T,
        "wq_t": np.asarray(L0_xattn_Wq).T,
        "bq": np.asarray(L0_xattn_bq),
        "wkv_t": np.concatenate([np.asarray(L0_xattn_Wk).T, np.asarray(L0_xattn_Wv).T], axis=1),
        "bkv": np.concatenate([np.asarray(L0_xattn_bk), np.asarray(L0_xattn_bv)]),
        "wr_t": np.asarray(L0_ffn_W_router).T,
        "br": np.asarray(L0_ffn_b_router),
        "w_in": np.asarray(L0_ffn_experts_inter),
        "w_out": np.asarray(L0_ffn_experts_out),
    }
    arrays = {name: np.ascontiguousarray(a) for name, a in arrays.items()}
    drams = [nc.dram_tensor(name + "_dram", a.shape, F32, kind="ExternalInput").ap() for name, a in arrays.items()]
    out = nc.dram_tensor("out_dram", (TOKENS + P, D), F32, kind="ExternalOutput").ap()
    slots = nc.dram_tensor("slots_dram", (SLOTS, ROW), F32).ap()
    build(nc, *drams, out, slots)
    r = run_bass_kernel_spmd(nc, [{name + "_dram": a for name, a in arrays.items()}], core_ids=[0])
    return r.results[0]["out_dram"][0:TOKENS].reshape(BATCHES, SEQ, D)
```

```python
import concourse.bass as bass
from concourse import mybir
from contextlib import ExitStack

F32 = mybir.dt.float32
F32R = mybir.dt.float32r
BF16 = mybir.dt.bfloat16
I32 = mybir.dt.int32
U32 = mybir.dt.uint32
ALU = mybir.AluOpType
ACT = mybir.ActivationFunctionType
AX = mybir.AxisListType

P = 128
BATCHES, SEQ, D = 128, 64, 128
HEADS, HD = 16, 8
EXPERTS, INNER, TOP_K = 8, 512, 2
TOKENS = BATCHES * SEQ
CAPACITY = -(-TOKENS * 5 // (EXPERTS * 4))
TILES = TOKENS // P
G = 4
CHUNKS = TILES // G
TOK = G * P
SLOTS = EXPERTS * CAPACITY
SLOT_TILES = CAPACITY // P
ROW_GATE, ROW_TOKEN, ROW = D, D + EXPERTS, D + EXPERTS + 1
NO_SLOT = 16384.0
LN_EPS, L2_EPS = 1e-5, 1e-12
HEAD = 4
RING = 4
IT = INNER // P
DUO = 2 * G
DVE_PER_TURN = 58
PAIR = 2
GROUPS = SLOT_TILES // PAIR
PG = PAIR * P
GROUP_HEAD = 2


class Chunk:

    def __init__(self, it, k):
        self.it, self.k = it, k

    def back(self, n):
        k = self.k - n
        return Chunk(self.it + (k // RING), k % RING)

    @property
    def number(self):
        return self.it * RING + self.k

    @property
    def known(self):
        return isinstance(self.it, int)

    def valid(self):
        return not self.known or 0 <= self.number < CHUNKS


def done(chunk):
    return chunk.number + (1 + HEAD)


class Group:

    def __init__(self, i, j):
        self.i, self.j = i + j // (2 * GROUPS), j % (2 * GROUPS)
        self.par, self.g = self.j // GROUPS, self.j % GROUPS
        self.b = self.j % 2
        self.expert = self.i * 2 + self.par

    def next(self, n):
        return Group(self.i, self.j + n)

    def valid(self):
        return not isinstance(self.i, int) or 0 <= self.i < EXPERTS // 2


def group_done(group):
    return group.i * (2 * GROUPS) + (group.j + 1 + GROUP_HEAD)


def group_steps(step):
    def run(engine):
        turns = EXPERTS // 2 - 1
        for j in range(-1, 2):
            step(Group(0, j))
        with engine.Fori(0, turns) as i:
            for j in range(2, 2 * GROUPS + 2):
                step(Group(i, j))
        for j in range(2, 2 * GROUPS + 2):
            step(Group(turns, j))
    return run


def duo_done(chunk):
    return chunk.it * (RING // 2) + (chunk.k // 2 + 1 + HEAD)


def may_be_full(chunk):
    return chunk.known and chunk.number * TOK * TOP_K >= SLOTS


class Local:

    def __init__(self, engine, sem):
        self.engine, self.sem, self.count, self.base = engine, sem, 0, 0

    def add(self, instruction):
        instruction.then_inc(self.sem, 1)
        self.count += 1

    def wait(self, apart=None):
        self.engine.wait_ge(self.sem, self.base + self.count)
        if apart is not None:
            self.engine.sem_inc(apart, 1)


def steps(engine, step, local=None, per_turn=0):
    first = RING + 1
    turns = (CHUNKS - 1 - first) // RING
    for s in range(-1, first):
        step(Chunk(s // RING, s % RING))
    start = local.count if local else 0
    with engine.Fori(1, 1 + turns) as i:
        if local:
            local.base, local.count = (i - 1) * per_turn, start
        for k in range(1, 1 + RING):
            step(Chunk(i, k).back(0))
        if local:
            assert local.count - start == per_turn, (local.count - start, per_turn)
    if local:
        local.base, local.count = 0, start + turns * per_turn
    for s in range(first + turns * RING, CHUNKS + 4):
        step(Chunk(s // RING, s % RING))


def build(nc, x, ctx_t, wq_t, bq, wkv_t, bkv, wr_t, br, w_in, w_out, out, slots):
    with ExitStack() as stack:
        def sb(name, shape, dt=F32):
            return stack.enter_context(nc.sbuf_tensor(name, shape, dt))

        def sem(name):
            return stack.enter_context(nc.semaphore(name))

        wq_sb = sb("wq_sb", [P, D])
        wkv_sb = sb("wkv_sb", [P, 2 * D])
        wr_sb = sb("wr_sb", [P, EXPERTS])
        bq_sb = sb("bq_sb", [P, 1])
        bkv_sb = sb("bkv_sb", [P, 2 * D])
        bkv_rest = sb("bkv_rest", [P, 2 * D])
        bkv_part = sb("bkv_part", [P, 3, 2 * D], BF16)
        bkv_rows = sb("bkv_rows", [P, 2 * D], BF16)
        br_sb = sb("br_sb", [P, EXPERTS])
        eps_sb = sb("eps_sb", [P, 1])
        ident = sb("ident", [P, P])
        head_mask = sb("head_mask", [P, D])
        before = sb("before", [P, P], BF16)
        ones = sb("ones", [P, P], BF16)
        iota8 = sb("iota8", [P, EXPERTS])
        slot_base = sb("slot_base", [P, EXPERTS])
        token_no = sb("token_no", [P, TILES], I32)
        empty_row = sb("empty_row", [P, ROW])
        x_sb = sb("x_sb", [P, RING, G, D])
        ct_sb = sb("ct_sb", [P, RING, TOK])
        xn2 = sb("xn2", [P, RING, G, D])
        rows = sb("rows", [P, RING, G, ROW])
        xn = sb("xn", [P, 2, G, D])
        xnt = sb("xnt", [P, TOK])
        qt = sb("qt", [P, 2, TOK])
        kvb = sb("kvb", [P, 2, G, 2, D])
        sq = sb("sq", [P, G, 2, D])
        ss = sb("ss", [P, G, 2, HEADS])
        kv_norm = sb("kv_norm", [P, G, 2, HEADS])
        key_scale = sb("key_scale", [P, G, HEADS])
        state = sb("state", [P, 2, G, D])
        x1 = sb("x1", [P, 2, G, D])
        x2t = sb("x2t", [P, TOK])
        st1 = sb("st1", [P, 2, G, 6])
        mv1 = sb("mv1", [P, 2, G, 2])
        sd1 = sb("sd1", [P, G])
        sc1 = sb("sc1", [P, 2, 2, G])
        st2 = sb("st2", [P, 2, G, 6])
        mv2 = sb("mv2", [P, 2, G, 2])
        sd2 = sb("sd2", [P, G])
        sc2 = sb("sc2", [P, 2, 2, G])
        logit = sb("logit", [P, DUO, EXPERTS])
        best = sb("best", [P, DUO, 8])
        best_no = sb("best_no", [P, DUO, 8], U32)
        shifted = sb("shifted", [P, DUO, EXPERTS])
        expo = sb("expo", [P, DUO, EXPERTS])
        total = sb("total", [P, DUO])
        prob = sb("prob", [P, DUO, EXPERTS])
        chosen = sb("chosen", [P, DUO, TOP_K, EXPERTS])
        either = sb("either", [P, DUO, EXPERTS])
        gates = sb("gates", [P, DUO, EXPERTS])
        routed = sb("routed", [P, DUO, EXPERTS], BF16)
        in_chunk = sb("in_chunk", [P, EXPERTS])
        earlier = sb("earlier", [P, 2, EXPERTS], BF16)
        fits = sb("fits", [P, DUO, EXPERTS])
        place = sb("place", [P, DUO, EXPERTS])
        place_k = sb("place_k", [P, DUO, TOP_K, EXPERTS])
        place_f = sb("place_f", [P, DUO, TOP_K])
        fewest = sb("fewest", [1, CHUNKS // 2], I32)
        place_no = sb("place_no", [P, 2, DUO * TOP_K], I32)
        wi_sb = sb("wi_sb", [P, 2, INNER])
        wo_sb = sb("wo_sb", [P, 2, IT * D])
        wi_hi = sb("wi_hi", [P, 2, INNER], F32R)
        wi_lo = sb("wi_lo", [P, 2, INNER], F32R)
        wo_hi = sb("wo_hi", [P, 2, IT * D], F32R)
        wo_lo = sb("wo_lo", [P, 2, IT * D], F32R)
        xg = sb("xg", [P, 2, SLOT_TILES, ROW])
        gate = sb("gate", [P, 2, SLOT_TILES])
        token = sb("token", [P, 2, SLOT_TILES], I32)
        xgt_hi = sb("xgt_hi", [P, 2, PG], F32R)
        xgt_lo = sb("xgt_lo", [P, 2, PG], F32R)
        hid_hi = sb("hid_hi", [P, 2, IT * PG], F32R)
        hid_lo = sb("hid_lo", [P, 2, IT * PG], F32R)
        yt = sb("yt", [P, 2, PG])
        y_sb = sb("y_sb", [P, 2, SLOT_TILES, D])

        ps0, ps1, ps2, ps3 = [stack.enter_context(nc.psum_tensor(f"ps{i}", [P, 1024], F32)) for i in range(4)]
        ps_kv = ps0[:, :].rearrange("p (g a d) -> p g a d", g=G, a=2)
        ps_state = ps1[:, :].rearrange("p (h g d) -> p h g d", h=2, g=G)
        ps_t, ps_q = ps2[:, 0:512], ps2[:, 512:1024]
        ps_o = ps3[:, 0:512].rearrange("p (g d) -> p g d", g=G)
        ps_logit = ps3[:, 512:512 + DUO * EXPERTS].rearrange("p (g e) -> p g e", g=DUO)
        ps_rank = ps3[:, 768:768 + DUO * EXPERTS].rearrange("p (g e) -> p g e", g=DUO)

        small_loaded = sem("small_loaded")
        consts_made = sem("consts_made")
        x_loaded = [sem(f"x_loaded{b}") for b in range(RING)]
        ct_loaded = [sem(f"ct_loaded{b}") for b in range(RING)]
        rows_filled = [sem(f"rows_filled{b}") for b in range(RING)]
        rows_sent = [sem(f"rows_sent{b}") for b in range(RING)]
        x1_stored = [sem(f"x1_stored{b}") for b in range(2)]
        dummies_stored = sem("dummies_stored")
        ln1_scaled, x_normed, x_turned, xnt_made = map(sem, ("ln1_scaled", "x_normed", "x_turned", "xnt_made"))
        kv_projected, q_projected, qt_made = map(sem, ("kv_projected", "q_projected", "qt_made"))
        v_made, kv_squared, kv_rooted, norms_ready, kn_made = map(
            sem, ("v_made", "kv_squared", "kv_rooted", "norms_ready", "kn_made"))
        bias_ready = sem("bias_ready")
        state_summed, state_made, attended, x1_made = map(
            sem, ("state_summed", "state_made", "attended", "x1_made"))
        ln1_var, ln1_root, ln2_var, ln2_root, ln2_scaled = map(
            sem, ("ln1_var", "ln1_root", "ln2_var", "ln2_root", "ln2_scaled"))
        rows_normed, rows_turned, x2t_made, logits_ready = map(
            sem, ("rows_normed", "rows_turned", "x2t_made", "logits_ready"))
        shift_ready, exp_ready, routed_ready, rank_ready, place_ready = map(
            sem, ("shift_ready", "exp_ready", "routed_ready", "rank_ready", "place_ready"))
        rank_read = sem("rank_read")
        dve_order = sem("dve_order")
        pool_order = sem("pool_order")
        waits_apart = sem("waits_apart")
        weights_loaded = [sem(f"weights_loaded{b}") for b in range(2)]
        xg_loaded = [sem(f"xg_loaded{b}") for b in range(2)]
        weights_high, weights_low = map(sem, ("weights_high", "weights_low"))
        group_turned, xgt_high, xgt_low, up_done, hid_high, hid_low = map(
            sem, ("group_turned", "xgt_high", "xgt_low", "up_done", "hid_high", "hid_low"))
        yt_made, y_turned = map(sem, ("yt_made", "y_turned"))
        down_done, y_made, rows_added, experts_added, gates_made = map(
            sem, ("down_done", "y_made", "rows_added", "experts_added", "gates_made"))

        x_c = x.rearrange("(c g p) d -> c p g d", g=G, p=P)
        out_c = out[0:TOKENS, :].rearrange("(c g p) d -> c p g d", g=G, p=P)
        slots_e = slots.rearrange("(e j p) r -> e p j r", e=EXPERTS, p=P)

        def head_start(engine, *sems):
            for s in sems:
                engine.sem_inc(s, HEAD)

        def group_head_start(engine, *sems):
            for s in sems:
                engine.sem_inc(s, GROUP_HEAD)

        block = stack.enter_context(nc.Block())

        @block.sync
        def _(sp):
            def load(c):
                if not c.valid():
                    return
                if not (c.known and c.number < RING):
                    sp.wait_ge(x1_made, done(c.back(RING)))
                    sp.wait_ge(kv_projected, done(c.back(RING)))
                if c.known:
                    x_src, ct_src = x_c[c.number], ctx_t[:, c.number * TOK:(c.number + 1) * TOK]
                else:
                    x_src = x_c[bass.ds(c.number, 1)].rearrange("c p g d -> (c p) g d")
                    ct_src = ctx_t[:, bass.ds(c.number * TOK, TOK)]
                sp.dma_start(x_sb[:, c.k], x_src).then_inc(x_loaded[c.k], 16)
                sp.dma_start(ct_sb[:, c.k, :], ct_src).then_inc(ct_loaded[c.k], 16)

            def store(c):
                if not c.valid():
                    return
                sp.wait_ge(x1_made, done(c))
                dst = out_c[c.number] if c.known else \
                    out_c[bass.ds(c.number, 1)].rearrange("c p g d -> (c p) g d")
                sp.dma_start(dst, x1[:, c.k % 2]).then_inc(x1_stored[c.k % 2], 16)

            def fill(c):
                if not c.valid():
                    return
                if not (c.known and c.number < RING):
                    sp.wait_ge(rows_sent[c.k], (c.it + 1) * (G * TOP_K * 16))
                    sp.sem_inc(waits_apart, 1)
                sp.wait_ge(rows_normed, done(c))
                sp.dma_start(rows[:, c.k, :, 0:D], xn2[:, c.k]).then_inc(rows_filled[c.k], 16)

            def step(s):
                load(s.back(-2))
                store(s.back(1))
                if s.k % 2 == 0:
                    fill(s.back(4))
                    fill(s.back(3))
                if s.known and s.number == 0:
                    sp.wait_ge(consts_made, 2)
                    sp.dma_start(out[TOKENS:TOKENS + P, :], empty_row[:, 0:D]).then_inc(dummies_stored, 16)
                    for par in range(2):
                        load_weights(0, par)

            def load_weights(i, par):
                e = i * 2 + par
                if isinstance(e, int):
                    up, down = w_in[e], w_out[e]
                else:
                    up = w_in[bass.ds(e, 1)].rearrange("e h i -> (e h) i")
                    down = w_out[bass.ds(e, 1)].rearrange("e i h -> (e i) h")
                sp.dma_start(wi_sb[:, par, :], up).then_inc(weights_loaded[par], 16)
                sp.dma_start(wo_sb[:, par, :].rearrange("p (t h) -> p t h", t=IT), down.rearrange("(t p) h -> p t h", p=P)).then_inc(weights_loaded[par], 16)

            def load_slots(i, par):
                e = i * 2 + par
                src = slots_e[e] if isinstance(e, int) else \
                    slots_e[bass.ds(e, 1)].rearrange("e p j r -> (e p) j r")
                sp.dma_start(xg[:, par], src).then_inc(xg_loaded[par], 16)

            sp.dma_start(wq_sb[:, :], wq_t).then_inc(small_loaded, 16)
            sp.dma_start(wkv_sb[:, :], wkv_t).then_inc(small_loaded, 16)
            sp.dma_start(wr_sb[:, :], wr_t).then_inc(small_loaded, 16)
            sp.dma_start(bq_sb[:, :], bq.rearrange("(p a) -> p a", a=1)).then_inc(small_loaded, 16)
            sp.dma_start(bkv_sb[:, :], bkv.rearrange("(a d) -> a d", a=1).broadcast_to([P, 2 * D])).then_inc(small_loaded, 16)
            sp.dma_start(br_sb[:, :], br.rearrange("(a d) -> a d", a=1).broadcast_to([P, EXPERTS])).then_inc(small_loaded, 16)
            for b in range(RING):
                sp.sem_inc(rows_filled[b], 16)
            load(Chunk(0, 0))
            steps(sp, step)
            for b in range(RING):
                sp.wait_ge(rows_sent[b], G * TOP_K * 16 * (CHUNKS // RING + 1))
            for par in range(2):
                load_slots(0, par)
            with sp.Fori(1, EXPERTS // 2) as i:
                for par in range(2):
                    sp.wait_ge(weights_low, i * 4 + (2 * par - 2))
                    load_weights(i, par)
                    sp.wait_ge(group_turned, group_done(Group(i - 1, par * GROUPS + GROUPS - 1)))
                    load_slots(i, par)

        @block.gpsimd
        def _(pool):
            order = Local(pool, pool_order)
            order.add(pool.memset(empty_row[:, :], 0.0))
            order.add(pool.memset(ident[:, :], 0.0))
            order.add(pool.memset(head_mask[:, :], 1.0))
            order.add(pool.memset(before[:, :], 1.0))
            pool.memset(ones[:, :], 1.0)
            pool.memset(eps_sb[:, :], LN_EPS)
            order.wait()
            order.add(pool.affine_select(out=ident[:, :], in_=ident[:, :], compare_op=ALU.not_equal, fill=1.0,
                                         base=0, pattern=[[-1, P]], channel_multiplier=1))
            order.add(pool.affine_select(out=head_mask[:, :], in_=head_mask[:, :], compare_op=ALU.is_ge, fill=0.0,
                                         base=0, pattern=[[-HD, HEADS], [0, HD]], channel_multiplier=1))
            order.wait()
            pool.affine_select(out=head_mask[:, :], in_=head_mask[:, :], compare_op=ALU.is_ge, fill=0.0,
                               base=HD - 1, pattern=[[HD, HEADS], [0, HD]], channel_multiplier=-1)
            pool.affine_select(out=before[:, :], in_=before[:, :], compare_op=ALU.is_gt, fill=0.0,
                               base=0, pattern=[[1, P]], channel_multiplier=-1)
            pool.iota(iota8[:, :], pattern=[[1, EXPERTS]], base=0, channel_multiplier=0,
                      allow_small_or_imprecise_dtypes=True)
            pool.iota(slot_base[:, :], pattern=[[CAPACITY, EXPERTS]], base=-int(NO_SLOT), channel_multiplier=0,
                      allow_small_or_imprecise_dtypes=True)
            pool.iota(token_no[:, :], pattern=[[P, TILES]], base=0, channel_multiplier=1)
            pool.iota(empty_row[:, ROW_TOKEN:ROW].bitcast(I32), pattern=[[0, 1]], base=TOKENS,
                      channel_multiplier=1).then_inc(pool_order, 1)
            order.count += 1
            order.wait()
            pool.drain().then_inc(consts_made, 2)
            pool.sem_inc(experts_added, 2)
            per = EXPERTS // RING
            for e in range(EXPERTS):
                pool.dma_start(slots_e[e], empty_row[:, None, :].broadcast_to([P, SLOT_TILES, ROW])) \
                    .then_inc(rows_sent[e // per], G * TOP_K * 16 // per)

            def scatter(s, first_only=False):
                for j in range(DUO * TOP_K):
                    c = s.back(5 - j // (G * TOP_K))
                    if first_only and j % (G * TOP_K):
                        continue
                    pool.indirect_dma_start(
                        slots[:, :], bass.IndirectOffsetOnAxis(
                            ap=place_no[:, c.k // 2, j:j + 1], axis=0),
                        rows[:, c.k, j // TOP_K % G, :], None, bounds_check=SLOTS - 1, oob_is_err=False,
                    ).then_inc(rows_sent[c.k], 16 * G * TOP_K if first_only else 16)

            def step(s):
                if s.k % 2 == 0 or not s.back(4).valid():
                    return
                pool.wait_ge(place_ready, duo_done(s.back(5)))
                for h in (5, 4):
                    pool.wait_ge(rows_filled[s.back(h).k], s.back(h).it * 16 + 32)
                pool.sem_inc(waits_apart, 1)
                if not may_be_full(s.back(5)):
                    scatter(s)
                else:
                    least = pool.value_load(fewest[0:1, s.back(5).number // 2:s.back(5).number // 2 + 1])
                    with pool.If(least < CAPACITY):
                        scatter(s)
                    with pool.Else():
                        scatter(s, first_only=True)

            for b in range(RING):
                pool.wait_ge(rows_sent[b], G * TOP_K * 16)
            steps(pool, step)

            for b in range(2):
                pool.wait_ge(x1_stored[b], 16 * (CHUNKS // 2))
            pool.wait_ge(dummies_stored, 16)
            with pool.Fori(0, EXPERTS // 2) as i:
                for par in range(2):
                    e = i * 2 + par
                    pool.wait_ge(gates_made, e + 1)
                    for g in range(GROUPS):
                        pool.wait_ge(y_made, group_done(Group(i, par * GROUPS + g)))
                        pool.sem_inc(waits_apart, 1)
                        for t in range(PAIR):
                            j = g * PAIR + t
                            pool.indirect_dma_start(
                                out[:, :], bass.IndirectOffsetOnAxis(
                                    ap=token[:, par, j:j + 1], axis=0),
                                y_sb[:, par, j, :], None, compute_op=ALU.add,
                            ).then_inc(rows_added, 16)
                    pool.wait_ge(rows_added, e * (16 * SLOT_TILES) + 16 * SLOT_TILES)
                    pool.sem_inc(experts_added, 1)

        @block.scalar
        def _(act):
            head_start(act, ln1_root, ln2_root, x_normed, xnt_made, qt_made, v_made, kv_squared, kv_rooted, rows_normed,
                       x2t_made, exp_ready)
            act.wait_ge(consts_made, 2)
            act.wait_ge(small_loaded, 16 * 6)

            def root1(c):
                if not c.valid():
                    return
                act.wait_ge(ln1_var, done(c))
                if not (c.known and c.number < 1):
                    act.wait_ge(ln1_scaled, done(c.back(1)))
                act.activation(sd1[:, :], mv1[:, c.k % 2, :, 1], ACT.Sqrt, bias=eps_sb[:, :]).then_inc(ln1_root, 1)

            def norm1(c):
                if not c.valid():
                    return
                act.wait_ge(ln1_scaled, done(c))
                if not (c.known and c.number < 2):
                    act.wait_ge(x_turned, done(c.back(2)))
                for g in range(G):
                    ins = act.activation(xn[:, c.k % 2, g, :], x_sb[:, c.k, g, :], ACT.Identity,
                                         scale=sc1[:, c.k % 2, 0, g:g + 1], bias=sc1[:, c.k % 2, 1, g:g + 1])
                ins.then_inc(x_normed, 1)

            def step(s):
                n, l = s.back(-1), s.back(2)
                if s.valid():
                    act.wait_ge(x_turned, done(s))
                    if not (s.known and s.number < 1):
                        act.wait_ge(q_projected, done(s.back(1)))
                    act.copy(xnt[:, :], ps_t).then_inc(xnt_made, 1)
                if l.valid():
                    act.wait_ge(ln2_var, done(l))
                    if not (l.known and l.number < 1):
                        act.wait_ge(ln2_scaled, done(l.back(1)))
                    act.activation(sd2[:, :], mv2[:, l.k % 2, :, 1], ACT.Sqrt, bias=eps_sb[:, :]).then_inc(ln2_root, 1)
                root1(n)
                if s.valid():
                    act.wait_ge(kv_projected, done(s))
                    if not (s.known and s.number < 1):
                        act.wait_ge(norms_ready, done(s.back(1)))
                    act.activation(sq[:, :, :, :], ps_kv, ACT.Square).then_inc(kv_squared, 1)
                if l.valid():
                    act.wait_ge(ln2_scaled, done(l))
                    if not (l.known and l.number < RING):
                        act.wait_ge(rows_filled[l.k], l.it * 16 + 16)
                    for g in range(G):
                        ins = act.activation(xn2[:, l.k, g, :], x1[:, l.k % 2, g, :], ACT.Identity,
                                             scale=sc2[:, l.k % 2, 0, g:g + 1], bias=sc2[:, l.k % 2, 1, g:g + 1])
                    ins.then_inc(rows_normed, 1)
                if s.valid():
                    act.wait_ge(norms_ready, done(s))
                    act.activation(kv_norm[:, :, :, :], ss[:, :, :, :], ACT.Sqrt).then_inc(kv_rooted, 1)
                    if not (s.known and s.number < 2):
                        act.wait_ge(state_summed, done(s.back(2)))
                    act.copy(kvb[:, s.k % 2, :, 1, :], ps_kv[:, :, 1, :]).then_inc(v_made, 1)
                    act.wait_ge(q_projected, done(s))
                    if not (s.known and s.number < 2):
                        act.wait_ge(attended, done(s.back(2)))
                    act.activation(qt[:, s.k % 2, :], ps_q, ACT.Identity, bias=bq_sb[:, :]).then_inc(qt_made, 1)
                if l.valid():
                    act.wait_ge(rows_turned, done(l))
                    if not (l.known and l.number < 1):
                        act.wait_ge(logits_ready, done(l.back(1)))
                    act.copy(x2t[:, :], ps_t).then_inc(x2t_made, 1)
                norm1(n)
                if s.k % 2 == 0 and s.back(4).valid():
                    act.wait_ge(shift_ready, duo_done(s.back(4)))
                    act.activation(expo[:, :, :], shifted[:, :, :], ACT.Exp).then_inc(exp_ready, 1)

            steps(act, step)
            group_head_start(act, xgt_high, hid_high, y_made, yt_made)

            def high_part(i, par, which):
                act.wait_ge(weights_loaded[par], i * 32 + 32)
                act.copy((wi_hi, wo_hi)[which][:, par, :], (wi_sb, wo_sb)[which][:, par, :]).then_inc(weights_high, 1)

            for which in range(2):
                high_part(0, 0, which)

            def b_step(n):
                t, y = n.next(1), n.next(-2)
                if y.valid():
                    act.wait_ge(down_done, group_done(y))
                    act.wait_ge(y_turned, group_done(y.next(-2)))
                    act.copy(yt[:, y.b, :], ps3[:, 512 * y.b:512 * y.b + PG]).then_inc(yt_made, 1)
                if t.valid():
                    act.wait_ge(group_turned, group_done(t))
                    act.wait_ge(up_done, group_done(t.next(-2)))
                    act.copy(xgt_hi[:, t.b, :], ps2[:, 512 * t.b:512 * t.b + PG]).then_inc(xgt_high, 1)
                if n.valid():
                    act.wait_ge(up_done, group_done(n))
                    act.wait_ge(down_done, group_done(n.next(-2)))
                    act.activation(hid_hi[:, n.b, :], [ps0, ps1][n.b][:, :], ACT.Relu).then_inc(hid_high, 1)
                if y.valid():
                    if y.g == 0:
                        act.wait_ge(gates_made, y.expert + 1)
                        act.wait_ge(experts_added, y.expert + 1)
                    act.wait_ge(y_turned, group_done(y))
                    for q in range(PAIR):
                        j = y.g * PAIR + q
                        ins = act.activation(y_sb[:, y.par, j, :],
                                             ps3[:, 512 * y.b + PG + P * q:512 * y.b + PG + P * (q + 1)],
                                             ACT.Copy, scale=gate[:, y.par, j:j + 1])
                    ins.then_inc(y_made, 1)
                e = n.next(GROUPS)
                if n.valid() and n.g in (1, 2) and e.valid():
                    high_part(e.i, e.par, n.g - 1)

            group_steps(b_step)(act)

        @block.vector
        def _(dve):
            order = Local(dve, dve_order)
            head_start(dve, ln1_var, ln1_scaled, norms_ready, kn_made, state_made, x1_made,
                       ln2_var, ln2_scaled, shift_ready, routed_ready, rank_read, place_ready)
            order.add(dve.memset(earlier[:, 0, :], 0.0))
            dve.wait_ge(consts_made, 2)
            dve.wait_ge(small_loaded, 16 * 6)

            left = bkv_sb
            for r in range(3):
                order.add(dve.tensor_copy(bkv_part[:, r, :], left[:, :]))
                order.wait()
                if r == 0:
                    order.add(dve.tensor_scalar(bkv_rows[:, :], bkv_part[:, r, :], ident[:, r:r + 1], None, ALU.mult))
                else:
                    order.add(dve.scalar_tensor_tensor(bkv_rows[:, :], bkv_part[:, r, :], ident[:, r:r + 1],
                                                       bkv_rows[:, :], ALU.mult, ALU.add))
                if r < 2:
                    order.add(dve.tensor_tensor(bkv_rest[:, :], left[:, :], bkv_part[:, r, :], ALU.subtract))
                    order.wait()
                    left = bkv_rest
            order.wait()
            dve.tensor_copy(bkv_rows[:, :], bkv_rows[:, :]).then_inc(bias_ready, 1)

            def spread(scalars):
                return scalars.broadcast_to([P, DUO, EXPERTS])

            def step(s):
                n, a, l = s.back(-1), s.back(1), s.back(2)
                gating = s.k % 2 == 0 and s.back(4).valid()
                placing = s.k % 2 == 1 and s.back(4).valid()

                if n.valid():
                    dve.wait_ge(x_loaded[n.k], (n.it + 1) * 16)
                    for g in range(G):
                        ins = dve.bn_stats(st1[:, n.k % 2, g, :], x_sb[:, n.k, g, :])
                    order.add(ins)
                if gating:
                    dve.wait_ge(logits_ready, done(s.back(3)))
                    order.add(dve.tensor_tensor(logit[:, :, :], ps_logit, spread(br_sb[:, None, :]), ALU.add))
                if l.valid():
                    dve.wait_ge(ln2_root, done(l))
                    order.add(dve.reciprocal(sc2[:, l.k % 2, 0, :], sd2[:, :]))
                if n.valid():
                    order.wait(waits_apart)
                    for g in range(G):
                        ins = dve.bn_aggr(mv1[:, n.k % 2, g, :], st1[:, n.k % 2, g, :])
                    ins.then_inc(ln1_var, 1)
                else:
                    order.wait()
                if l.valid():
                    dve.scalar_tensor_tensor(sc2[:, l.k % 2, 1, :], mv2[:, l.k % 2, :, 0], -1.0,
                                             sc2[:, l.k % 2, 0, :], ALU.mult, ALU.mult).then_inc(ln2_scaled, 1)
                if gating:
                    order.wait(waits_apart)
                    for g in range(DUO):
                        ins = dve.max(best[:, g, :], logit[:, g, :])
                    order.add(ins)
                if n.valid():
                    dve.wait_ge(ln1_root, done(n))
                    order.add(dve.reciprocal(sc1[:, n.k % 2, 0, :], sd1[:, :]))
                if gating:
                    order.wait(waits_apart)
                    dve.tensor_tensor(shifted[:, :, :], logit[:, :, :], spread(best[:, :, 0:1]),
                                      ALU.subtract).then_inc(shift_ready, 1)
                    for g in range(DUO):
                        ins = dve.max_index(best_no[:, g, :], best[:, g, :], logit[:, g, :])
                    order.add(ins)
                elif n.valid():
                    order.wait()
                if n.valid():
                    dve.scalar_tensor_tensor(sc1[:, n.k % 2, 1, :], mv1[:, n.k % 2, :, 0], -1.0,
                                             sc1[:, n.k % 2, 0, :], ALU.mult, ALU.mult).then_inc(ln1_scaled, 1)
                if s.valid():
                    dve.wait_ge(kv_squared, done(s))
                    order.add(dve.tensor_reduce(ss[:, :, :, :],
                                                sq[:, :, :, :].rearrange("p g a (h i) -> p g a h i", i=HD),
                                                AX.X, ALU.add))
                if placing:
                    dve.wait_ge(rank_ready, duo_done(s.back(5)))
                    order.add(dve.scalar_tensor_tensor(fits[:, :, :], ps_rank, float(CAPACITY), routed[:, :, :],
                                                       ALU.is_lt, ALU.mult))
                if s.valid():
                    order.wait()
                    dve.tensor_scalar(ss[:, :, :, :], ss[:, :, :, :], L2_EPS * L2_EPS, None,
                                      ALU.max).then_inc(norms_ready, 1)
                if placing:
                    order.add(dve.tensor_tensor(place[:, :, :], ps_rank, spread(slot_base[:, None, :]), ALU.add))
                    if may_be_full(s.back(5)):
                        dve.tensor_reduce(fewest[0:1, s.back(5).number // 2:s.back(5).number // 2 + 1], ps_rank[0:1, 0, :], AX.X, ALU.min)
                if a.valid():
                    dve.wait_ge(state_summed, done(a))
                    if not (a.known and a.number < 1):
                        dve.wait_ge(attended, done(a.back(1)))
                    dve.tensor_tensor(state[:, :, :, :].rearrange("p h g d -> p (h g) d"),
                                      ps_state.rearrange("p h g d -> p (h g) d"),
                                      head_mask[:, None, :].broadcast_to([P, 2 * G, D]),
                                      ALU.mult).then_inc(state_made, 1)
                if placing:
                    order.wait()
                    dve.tensor_tensor(place[:, :, :], place[:, :, :], fits[:, :, :], ALU.mult).then_inc(rank_read, 1)
                if s.valid():
                    dve.wait_ge(kv_rooted, done(s))
                    order.add(dve.tensor_tensor(key_scale[:, :, :], kv_norm[:, :, 0, :], kv_norm[:, :, 1, :], ALU.mult))
                if placing:
                    dve.wait_ge(rank_read, duo_done(s.back(5)))
                    order.add(dve.tensor_tensor(
                        place_k[:, :, :, :], chosen[:, :, :, :],
                        place[:, :, None, :].broadcast_to([P, DUO, TOP_K, EXPERTS]), ALU.mult))
                if s.valid():
                    order.wait()
                    order.add(dve.reciprocal(key_scale[:, :, :], key_scale[:, :, :]))
                if placing:
                    if not s.valid():
                        order.wait()
                    order.add(dve.tensor_reduce(place_f[:, :, :], place_k[:, :, :, :], AX.X, ALU.add))
                if s.valid():
                    order.wait()
                    if not (s.known and s.number < 2):
                        dve.wait_ge(state_summed, done(s.back(2)))
                    dve.wait_ge(v_made, done(s))
                    dve.tensor_tensor(kvb[:, s.k % 2, :, 0, :].rearrange("p g (h i) -> p g h i", i=HD),
                                      ps_kv[:, :, 0, :].rearrange("p g (h i) -> p g h i", i=HD),
                                      key_scale[:, :, :, None].broadcast_to([P, G, HEADS, HD]),
                                      ALU.mult).then_inc(kn_made, 1)
                if placing:
                    for h in range(2):
                        c = s.back(5 - h)
                        if not (c.known and c.number < RING):
                            dve.wait_ge(rows_sent[c.k], (c.it + 1) * (G * TOP_K * 16))
                        dve.tensor_copy(rows[:, c.k, :, ROW_GATE:ROW_TOKEN], gates[:, G * h:G * (h + 1), :])
                        tiles = token_no[:, c.number * G:c.number * G + G] if c.known else \
                            token_no[:, bass.ds(c.number * G, G)]
                        dve.tensor_copy(rows[:, c.k, :, ROW_TOKEN].bitcast(I32), tiles)
                    if not s.valid():
                        order.wait()
                    dve.tensor_scalar(place_no[:, s.back(5).k // 2, :], place_f[:, :, :].rearrange("p g k -> p (g k)"),
                                      NO_SLOT, None, ALU.add).then_inc(place_ready, 1)
                if a.valid():
                    dve.wait_ge(attended, done(a))
                    if not (a.known and a.number < 2):
                        dve.wait_ge(x1_stored[a.k % 2], (a.it * RING + a.k - a.k % 2) * 8)
                        dve.wait_ge(rows_normed, done(a.back(2)))
                    dve.tensor_tensor(x1[:, a.k % 2], x_sb[:, a.k], ps_o, ALU.add).then_inc(x1_made, 1)
                if gating:
                    order.wait()
                    order.add(dve.tensor_tensor(
                        chosen[:, :, :, :], best_no[:, :, 0:TOP_K, None].broadcast_to([P, DUO, TOP_K, EXPERTS]),
                        iota8[:, None, None, :].broadcast_to([P, DUO, TOP_K, EXPERTS]), ALU.is_equal))
                if a.valid():
                    dve.wait_ge(x1_made, done(a))
                    for g in range(G):
                        ins = dve.bn_stats(st2[:, a.k % 2, g, :], x1[:, a.k % 2, g, :])
                    order.add(ins)
                if gating:
                    dve.wait_ge(exp_ready, duo_done(s.back(4)))
                    order.add(dve.tensor_reduce(total[:, :], expo[:, :, :], AX.X, ALU.add))
                if a.valid():
                    order.wait(waits_apart)
                    for g in range(G):
                        ins = dve.bn_aggr(mv2[:, a.k % 2, g, :], st2[:, a.k % 2, g, :])
                    ins.then_inc(ln2_var, 1)
                if gating:
                    order.wait()
                    order.add(dve.reciprocal(total[:, :], total[:, :]))
                    order.add(dve.tensor_tensor(either[:, :, :], chosen[:, :, 0, :], chosen[:, :, 1, :], ALU.add))
                    order.wait()
                    order.add(dve.tensor_tensor(prob[:, :, :], expo[:, :, :], spread(total[:, :, None]), ALU.mult))
                    order.wait()
                    order.add(dve.tensor_tensor(gates[:, :, :], prob[:, :, :], either[:, :, :], ALU.mult))
                    order.wait()
                    dve.tensor_scalar(routed[:, :, :], gates[:, :, :], 0.0, None, ALU.is_gt).then_inc(routed_ready, 1)
                    dve.wait_ge(routed_ready, duo_done(s.back(4)))
                    order.add(dve.tensor_reduce(in_chunk[:, :], routed[:, :, :].rearrange("p g e -> p e g"),
                                                AX.X, ALU.add))
                    duo = s.back(4).k // 2
                    order.wait()
                    order.add(dve.tensor_tensor(earlier[:, 1 - duo, :], earlier[:, duo, :], in_chunk[:, :], ALU.add))

            steps(dve, step, order, DVE_PER_TURN)

            group_head_start(dve, xgt_low, hid_low)

            def low_part(e, par, which):
                hi, raw, lo = (wi_hi, wi_sb, wi_lo) if which == 0 else (wo_hi, wo_sb, wo_lo)
                dve.wait_ge(weights_high, e * 2 + (1 + which))
                dve.tensor_tensor(lo[:, par, :], raw[:, par, :], hi[:, par, :].bitcast(F32),
                                  ALU.subtract).then_inc(weights_low, 1)

            for which in range(2):
                low_part(0, 0, which)

            def b_step(n):
                t = n.next(1)
                if t.valid():
                    if t.g == 0:
                        dve.wait_ge(xg_loaded[t.par], t.i * 16 + 16)
                        column = ROW_GATE + t.expert
                        src = xg[:, t.par, :, column] if isinstance(column, int) else \
                            xg[:, t.par, :, bass.ds(column, 1)].rearrange("p j a -> p (j a)")
                        dve.tensor_copy(gate[:, t.par, :], src)
                        dve.wait_ge(experts_added, t.expert + 1)
                        dve.tensor_copy(token[:, t.par, :], xg[:, t.par, :, ROW_TOKEN].bitcast(I32)).then_inc(gates_made, 1)
                    dve.wait_ge(xgt_high, group_done(t))
                    dve.tensor_tensor(xgt_lo[:, t.b, :], ps2[:, 512 * t.b:512 * t.b + PG],
                                      xgt_hi[:, t.b, :].bitcast(F32), ALU.subtract).then_inc(xgt_low, 1)
                if n.valid():
                    dve.wait_ge(hid_high, group_done(n))
                    dve.wait_ge(down_done, group_done(n.next(-2)))
                    dve.scalar_tensor_tensor(hid_lo[:, n.b, :], [ps0, ps1][n.b][:, :], 0.0,
                                             hid_hi[:, n.b, :].bitcast(F32), ALU.max,
                                             ALU.subtract).then_inc(hid_low, 1)
                e = n.next(GROUPS)
                if n.valid() and n.g in (1, 2) and e.valid():
                    low_part(e.expert, e.par, n.g - 1)

            group_steps(b_step)(dve)

        @block.tensor
        def _(pe):
            head_start(pe, x_turned, kv_projected, q_projected, state_summed, attended, rows_turned, logits_ready,
                       rank_ready)
            pe.wait_ge(consts_made, 2)
            pe.wait_ge(small_loaded, 16 * 6)
            pe.wait_ge(bias_ready, 1)

            def step(s):
                n, a, l = s.back(-1), s.back(1), s.back(2)
                if s.valid():
                    pe.wait_ge(ct_loaded[s.k], (s.it + 1) * 16)
                    if not (s.known and s.number < 1):
                        pe.wait_ge(kn_made, done(s.back(1)))
                        pe.wait_ge(v_made, done(s.back(1)))
                    for g in range(G):
                        bank = ps0[:, 256 * g:256 * (g + 1)]
                        pe.matmul(bank, ct_sb[:, s.k, P * g:P * (g + 1)], wkv_sb[:, :], start=True, stop=False)
                        ins = pe.matmul(bank, ones[:, :], bkv_rows[:, :], start=False, stop=True)
                    ins.then_inc(kv_projected, 1)
                if a.valid():
                    pe.wait_ge(kn_made, done(a))
                    pe.wait_ge(v_made, done(a))
                    if not (a.known and a.number < 1):
                        pe.wait_ge(state_made, done(a.back(1)))
                    for g in range(G):
                        for h in range(2):
                            half = slice(SEQ * h, SEQ * (h + 1))
                            ins = pe.matmul(ps_state[:, h, g, :], kvb[half, a.k % 2, g, 0, :], kvb[half, a.k % 2, g, 1, :],
                                            start=True, stop=True)
                    ins.then_inc(state_summed, 1)
                if s.k % 2 == 1 and s.back(4).valid():
                    r = s.back(5)
                    pe.wait_ge(routed_ready, duo_done(r))
                    pe.matmul(ps_rank, before[:, :], routed[:, :, :], start=True, stop=False)
                    for g in range(1, DUO):
                        pe.matmul(ps_rank[:, g:DUO, :], ones[:, :], routed[:, 0:DUO - g, :], start=False, stop=False)
                    pe.matmul(ps_rank, ones[:, :], earlier[:, r.k // 2, None, :].broadcast_to([P, DUO, EXPERTS]),
                              start=False, stop=True).then_inc(rank_ready, 1)
                if s.valid():
                    pe.wait_ge(xnt_made, done(s))
                    if not (s.known and s.number < 1):
                        pe.wait_ge(qt_made, done(s.back(1)))
                    pe.matmul(ps_q, wq_sb[:, :], xnt[:, :], start=True, stop=True).then_inc(q_projected, 1)
                if l.valid():
                    pe.wait_ge(rows_normed, done(l))
                    if not (s.known and not s.valid()):
                        pe.wait_ge(xnt_made, done(s))
                    for g in range(G):
                        ins = pe.transpose(ps_t[:, P * g:P * (g + 1)], xn2[:, l.k, g, :], ident[:, :])
                    ins.then_inc(rows_turned, 1)
                if a.valid():
                    pe.wait_ge(qt_made, done(a))
                    pe.wait_ge(state_made, done(a))
                    if not (a.known and a.number < 1):
                        pe.wait_ge(x1_made, done(a.back(1)))
                    for g in range(G):
                        for h in range(2):
                            tokens = slice(P * g + SEQ * h, P * g + SEQ * (h + 1))
                            ins = pe.matmul(ps_o[SEQ * h:SEQ * (h + 1), g, :], qt[:, a.k % 2, tokens], state[:, h, g, :],
                                            start=True, stop=True)
                    ins.then_inc(attended, 1)
                if l.valid():
                    pe.wait_ge(x2t_made, done(l))
                    if s.k % 2 == 0 and s.back(4).valid():
                        pe.wait_ge(shift_ready, duo_done(s.back(4)))
                    if s.k % 2 == 1 and s.back(4).valid():
                        pe.wait_ge(rank_read, duo_done(s.back(5)))
                    for g in range(G):
                        ins = pe.matmul(ps_logit[:, l.k % 2 * G + g, :], x2t[:, P * g:P * (g + 1)], wr_sb[:, :], start=True, stop=True)
                    ins.then_inc(logits_ready, 1)
                if n.valid():
                    pe.wait_ge(x_normed, done(n))
                    if l.valid():
                        pe.wait_ge(x2t_made, done(l))
                    elif s.valid():
                        pe.wait_ge(xnt_made, done(s))
                    for g in range(G):
                        ins = pe.transpose(ps_t[:, P * g:P * (g + 1)], xn[:, n.k % 2, g, :], ident[:, :])
                    ins.then_inc(x_turned, 1)

            steps(pe, step)

            group_head_start(pe, group_turned, up_done, down_done, y_turned)

            def b_step(n):
                t, m, y = n.next(1), n.next(-1), n.next(-2)
                if t.valid():
                    if t.g == 0:
                        pe.wait_ge(xg_loaded[t.par], t.i * 16 + 16)
                    pe.wait_ge(xgt_low, group_done(t.next(-2)))
                    for q in range(PAIR):
                        ins = pe.transpose(ps2[:, 512 * t.b + P * q:512 * t.b + P * (q + 1)],
                                           xg[:, t.par, t.g * PAIR + q, 0:D], ident[:, :])
                    ins.then_inc(group_turned, 1)
                if n.valid():
                    if n.g == 0:
                        pe.wait_ge(weights_low, n.expert * 2 + 2)
                    pe.wait_ge(xgt_low, group_done(n))
                    pe.wait_ge(hid_low, group_done(n.next(-2)))
                    for t in range(IT):
                        bank = [ps0, ps1][n.b][:, PG * t:PG * (t + 1)]
                        w_hi, w_lo = (w[:, n.par, P * t:P * (t + 1)] for w in (wi_hi, wi_lo))
                        pe.matmul(bank, w_hi, xgt_hi[:, n.b, :], start=True, stop=False)
                        pe.matmul(bank, w_hi, xgt_lo[:, n.b, :], start=False, stop=False)
                        ins = pe.matmul(bank, w_lo, xgt_hi[:, n.b, :], start=False, stop=True)
                    ins.then_inc(up_done, 1)
                if y.valid():
                    pe.wait_ge(yt_made, group_done(y))
                    pe.wait_ge(y_made, group_done(y.next(-2)))
                    for q in range(PAIR):
                        ins = pe.transpose(ps3[:, 512 * y.b + PG + P * q:512 * y.b + PG + P * (q + 1)],
                                           yt[:, y.b, P * q:P * (q + 1)], ident[:, :])
                    ins.then_inc(y_turned, 1)
                if m.valid():
                    pe.wait_ge(hid_low, group_done(m))
                    pe.wait_ge(y_made, group_done(m.next(-2)))
                    bank = ps3[:, 512 * m.b:512 * m.b + PG]
                    for t in range(IT):
                        h_hi, h_lo = (h[:, m.b, PG * t:PG * (t + 1)] for h in (hid_hi, hid_lo))
                        w_hi, w_lo = (w[:, m.par, D * t:D * (t + 1)] for w in (wo_hi, wo_lo))
                        pe.matmul(bank, w_hi, h_hi, start=(t == 0), stop=False)
                        pe.matmul(bank, w_hi, h_lo, start=False, stop=False)
                        ins = pe.matmul(bank, w_lo, h_hi, start=False, stop=(t == IT - 1))
                    ins.then_inc(down_done, 1)

            group_steps(b_step)(pe)


def kernel(x, ctx_1024, L0_xattn_Wq, L0_xattn_bq, L0_xattn_Wk, L0_xattn_bk, L0_xattn_Wv, L0_xattn_bv,
           L0_ffn_W_router, L0_ffn_b_router, L0_ffn_experts_inter, L0_ffn_experts_out):
    import numpy as np
    import concourse.bacc as bacc
    from concourse.bass_utils import run_bass_kernel_spmd

    nc = bacc.Bacc("TRN2", target_bir_lowering=False, num_devices=1)
    arrays = {
        "x": np.asarray(x).reshape(TOKENS, D),
        "ctx_t": np.asarray(ctx_1024).reshape(TOKENS, D).T,
        "wq_t": np.asarray(L0_xattn_Wq).T,
        "bq": np.asarray(L0_xattn_bq),
        "wkv_t": np.concatenate([np.asarray(L0_xattn_Wk).T, np.asarray(L0_xattn_Wv).T], axis=1),
        "bkv": np.concatenate([np.asarray(L0_xattn_bk), np.asarray(L0_xattn_bv)]),
        "wr_t": np.asarray(L0_ffn_W_router).T,
        "br": np.asarray(L0_ffn_b_router),
        "w_in": np.asarray(L0_ffn_experts_inter),
        "w_out": np.asarray(L0_ffn_experts_out),
    }
    arrays = {name: np.ascontiguousarray(a) for name, a in arrays.items()}
    drams = [nc.dram_tensor(name + "_dram", a.shape, F32, kind="ExternalInput").ap() for name, a in arrays.items()]
    out = nc.dram_tensor("out_dram", (TOKENS + P, D), F32, kind="ExternalOutput").ap()
    slots = nc.dram_tensor("slots_dram", (SLOTS, ROW), F32).ap()
    build(nc, *drams, out, slots)
    r = run_bass_kernel_spmd(nc, [{name + "_dram": a for name, a in arrays.items()}], core_ids=[0])
    return r.results[0]["out_dram"][0:TOKENS].reshape(BATCHES, SEQ, D)
```

```python
import concourse.bass as bass
from concourse import mybir
from contextlib import ExitStack

F32 = mybir.dt.float32
F32R = mybir.dt.float32r
BF16 = mybir.dt.bfloat16
I32 = mybir.dt.int32
U32 = mybir.dt.uint32
ALU = mybir.AluOpType
ACT = mybir.ActivationFunctionType
AX = mybir.AxisListType

P = 128
BATCHES, SEQ, D = 128, 64, 128
HEADS, HD = 16, 8
EXPERTS, INNER, TOP_K = 8, 512, 2
TOKENS = BATCHES * SEQ
CAPACITY = -(-TOKENS * 5 // (EXPERTS * 4))
TILES = TOKENS // P
G = 4
CHUNKS = TILES // G
TOK = G * P
SLOTS = EXPERTS * CAPACITY
SLOT_TILES = CAPACITY // P
ROW_GATE, ROW_TOKEN, ROW = D, D + EXPERTS, D + EXPERTS + 1
NO_SLOT = 16384.0
LN_EPS, L2_EPS = 1e-5, 1e-12
HEAD = 4
RING = 4
IT = INNER // P
DUO = 2 * G
DVE_PER_TURN = 54
PAIR = 2
GROUPS = SLOT_TILES // PAIR
PG = PAIR * P
GROUP_HEAD = 2


class Chunk:

    def __init__(self, it, k):
        self.it, self.k = it, k

    def back(self, n):
        k = self.k - n
        return Chunk(self.it + (k // RING), k % RING)

    @property
    def number(self):
        return self.it * RING + self.k

    @property
    def known(self):
        return isinstance(self.it, int)

    def valid(self):
        return not self.known or 0 <= self.number < CHUNKS


def done(chunk):
    return chunk.number + (1 + HEAD)


class Group:

    def __init__(self, i, j):
        self.i, self.j = i + j // (2 * GROUPS), j % (2 * GROUPS)
        self.par, self.g = self.j // GROUPS, self.j % GROUPS
        self.b = self.j % 2
        self.expert = self.i * 2 + self.par

    def next(self, n):
        return Group(self.i, self.j + n)

    def valid(self):
        return not isinstance(self.i, int) or 0 <= self.i < EXPERTS // 2


def group_done(group):
    return group.i * (2 * GROUPS) + (group.j + 1 + GROUP_HEAD)


def group_steps(step):
    def run(engine):
        turns = EXPERTS // 2 - 1
        for j in range(-1, 2):
            step(Group(0, j))
        with engine.Fori(0, turns) as i:
            for j in range(2, 2 * GROUPS + 2):
                step(Group(i, j))
        for j in range(2, 2 * GROUPS + 2):
            step(Group(turns, j))
    return run


def duo_done(chunk):
    return chunk.it * (RING // 2) + (chunk.k // 2 + 1 + HEAD)


def may_be_full(chunk):
    return chunk.known and chunk.number * TOK * TOP_K >= SLOTS


class Local:

    def __init__(self, engine, sem):
        self.engine, self.sem, self.count, self.base, self.named = engine, sem, 0, 0, {}

    def add(self, instruction, name=None):
        instruction.then_inc(self.sem, 1)
        self.count += 1
        self.named[name] = self.count

    def wait(self, name=None, apart=None):
        self.engine.wait_ge(self.sem, self.base + (self.named[name] if name else self.count))
        if apart is not None:
            self.engine.sem_inc(apart, 1)


def steps(engine, step, local=None, per_turn=0):
    first = RING + 1
    turns = (CHUNKS - 1 - first) // RING
    for s in range(-1, first):
        step(Chunk(s // RING, s % RING))
    start = local.count if local else 0
    with engine.Fori(1, 1 + turns) as i:
        if local:
            local.base, local.count = (i - 1) * per_turn, start
        for k in range(1, 1 + RING):
            step(Chunk(i, k).back(0))
        if local:
            assert local.count - start == per_turn, (local.count - start, per_turn)
    if local:
        local.base, local.count = 0, start + turns * per_turn
        local.named = {name: at + (turns - 1) * per_turn for name, at in local.named.items()}
    for s in range(first + turns * RING, CHUNKS + 4):
        step(Chunk(s // RING, s % RING))


def build(nc, x, ctx_t, wq_t, bq, wkv_t, bkv, wr_t, br, w_in, w_out, out, slots):
    with ExitStack() as stack:
        def sb(name, shape, dt=F32):
            return stack.enter_context(nc.sbuf_tensor(name, shape, dt))

        def sem(name):
            return stack.enter_context(nc.semaphore(name))

        wq_sb = sb("wq_sb", [P, D])
        wkv_sb = sb("wkv_sb", [P, 2 * D])
        wr_sb = sb("wr_sb", [P, EXPERTS])
        bq_sb = sb("bq_sb", [P, 1])
        bkv_sb = sb("bkv_sb", [P, 2 * D])
        bkv_rest = sb("bkv_rest", [P, 2 * D])
        bkv_part = sb("bkv_part", [P, 3, 2 * D], BF16)
        bkv_rows = sb("bkv_rows", [P, 2 * D], BF16)
        br_sb = sb("br_sb", [P, EXPERTS])
        eps_sb = sb("eps_sb", [P, 1])
        unused = sb("unused", [P, 1])
        ident = sb("ident", [P, P])
        head_mask = sb("head_mask", [P, D])
        before = sb("before", [P, P], BF16)
        ones = sb("ones", [P, P], BF16)
        iota8 = sb("iota8", [P, EXPERTS])
        slot_base = sb("slot_base", [P, EXPERTS])
        token_no = sb("token_no", [P, TILES], I32)
        empty_row = sb("empty_row", [P, ROW])
        x_sb = sb("x_sb", [P, RING, G, D])
        ct_sb = sb("ct_sb", [P, RING, TOK])
        xn2 = sb("xn2", [P, RING, G, D])
        rows = sb("rows", [P, RING, G, ROW])
        xn = sb("xn", [P, 2, G, D])
        xnt = sb("xnt", [P, TOK])
        qt = sb("qt", [P, 2, TOK])
        kvb = sb("kvb", [P, 2, G, 2, D])
        sq = sb("sq", [P, G, 2, D])
        ss = sb("ss", [P, G, 2, HEADS])
        kv_norm = sb("kv_norm", [P, G, 2, HEADS])
        key_scale = sb("key_scale", [P, G, HEADS])
        state = sb("state", [P, 2, G, D])
        x1 = sb("x1", [P, 2, G, D])
        x2t = sb("x2t", [P, TOK])
        sums = sb("sums", [P, 2, 2, G, 6])
        mean_var = sb("mean_var", [P, 2, 2, G, 2])
        std = sb("std", [P, 2, G])
        scales = sb("scales", [P, 2, 2, 2, G])
        logit = sb("logit", [P, DUO, EXPERTS])
        best = sb("best", [P, DUO, 8])
        best_no = sb("best_no", [P, DUO, 8], U32)
        shifted = sb("shifted", [P, DUO, EXPERTS])
        expo = sb("expo", [P, DUO, EXPERTS])
        total = sb("total", [P, DUO])
        prob = sb("prob", [P, DUO, EXPERTS])
        chosen = sb("chosen", [P, DUO, TOP_K, EXPERTS])
        either = sb("either", [P, DUO, EXPERTS])
        routed = sb("routed", [P, DUO, EXPERTS], BF16)
        in_chunk = sb("in_chunk", [P, EXPERTS])
        earlier = sb("earlier", [P, 2, EXPERTS], BF16)
        fits = sb("fits", [P, DUO, EXPERTS])
        place = sb("place", [P, DUO, EXPERTS])
        place_k = sb("place_k", [P, DUO, TOP_K, EXPERTS])
        place_f = sb("place_f", [P, DUO, TOP_K])
        fewest = sb("fewest", [1, CHUNKS // 2], I32)
        place_no = sb("place_no", [P, 2, DUO * TOP_K], I32)
        wi_sb = sb("wi_sb", [P, 2, INNER])
        wo_sb = sb("wo_sb", [P, 2, IT * D])
        wi_hi = sb("wi_hi", [P, 2, INNER], F32R)
        wi_lo = sb("wi_lo", [P, 2, INNER], F32R)
        wo_hi = sb("wo_hi", [P, 2, IT * D], F32R)
        wo_lo = sb("wo_lo", [P, 2, IT * D], F32R)
        xg = sb("xg", [P, 2, SLOT_TILES, ROW])
        gate = sb("gate", [P, 2, SLOT_TILES])
        token = sb("token", [P, 2, SLOT_TILES], I32)
        xgt_hi = sb("xgt_hi", [P, 2, PG], F32R)
        xgt_lo = sb("xgt_lo", [P, 2, PG], F32R)
        hid_hi = sb("hid_hi", [P, 2, IT * PG], F32R)
        hid_lo = sb("hid_lo", [P, 2, IT * PG], F32R)
        yt = sb("yt", [P, 2, PG])
        y_sb = sb("y_sb", [P, 2, SLOT_TILES, D])

        ps0, ps1, ps2, ps3 = [stack.enter_context(nc.psum_tensor(f"ps{i}", [P, 1024], F32)) for i in range(4)]
        ps_kv = ps0[:, :].rearrange("p (g a d) -> p g a d", g=G, a=2)
        ps_state = ps1[:, :].rearrange("p (h g d) -> p h g d", h=2, g=G)
        ps_t, ps_q = ps2[:, 0:512], ps2[:, 512:1024]
        ps_o = ps3[:, 0:512].rearrange("p (g d) -> p g d", g=G)
        ps_logit = ps3[:, 512:512 + DUO * EXPERTS].rearrange("p (g e) -> p g e", g=DUO)
        ps_rank = ps3[:, 768:768 + DUO * EXPERTS].rearrange("p (g e) -> p g e", g=DUO)

        ps_last = ps3[:, 896:896 + EXPERTS]

        small_loaded = sem("small_loaded")
        kv_consts_loaded = sem("kv_consts_loaded")
        consts_made = sem("consts_made")
        x_loaded = [sem(f"x_loaded{b}") for b in range(RING)]
        ct_loaded = [sem(f"ct_loaded{b}") for b in range(RING)]
        rows_filled = [sem(f"rows_filled{b}") for b in range(RING)]
        rows_sent = [sem(f"rows_sent{b}") for b in range(RING)]
        x1_stored = [sem(f"x1_stored{b}") for b in range(2)]
        dummies_stored = sem("dummies_stored")
        x_normed, x_turned, xnt_made = map(sem, ("x_normed", "x_turned", "xnt_made"))
        kv_projected, q_projected, qt_made = map(sem, ("kv_projected", "q_projected", "qt_made"))
        v_made, kv_squared, kv_rooted, norms_ready, kn_made = map(
            sem, ("v_made", "kv_squared", "kv_rooted", "norms_ready", "kn_made"))
        bias_ready = sem("bias_ready")
        state_summed, state_made, attended, x1_made = map(
            sem, ("state_summed", "state_made", "attended", "x1_made"))
        var_ready, std_ready, scales_ready = map(sem, ("var_ready", "std_ready", "scales_ready"))
        rows_normed, rows_turned, x2t_made, logits_ready = map(
            sem, ("rows_normed", "rows_turned", "x2t_made", "logits_ready"))
        shift_ready, exp_ready, routed_ready, rank_ready, place_ready = map(
            sem, ("shift_ready", "exp_ready", "routed_ready", "rank_ready", "place_ready"))
        rank_read = sem("rank_read")
        last_summed, last_counted, slots_ready = map(sem, ("last_summed", "last_counted", "slots_ready"))
        dve_order = sem("dve_order")
        pool_order = sem("pool_order")
        waits_apart = sem("waits_apart")
        weights_loaded = [sem(f"weights_loaded{b}") for b in range(2)]
        xg_begun = [sem(f"xg_begun{b}") for b in range(2)]
        xg_loaded = [sem(f"xg_loaded{b}") for b in range(2)]
        weights_high, weights_low = map(sem, ("weights_high", "weights_low"))
        group_turned, xgt_high, xgt_low, up_done, hid_high, hid_low = map(
            sem, ("group_turned", "xgt_high", "xgt_low", "up_done", "hid_high", "hid_low"))
        yt_made, y_turned = map(sem, ("yt_made", "y_turned"))
        down_done, y_made, rows_added, experts_added, gates_made = map(
            sem, ("down_done", "y_made", "rows_added", "experts_added", "gates_made"))

        x_c = x.rearrange("(c g p) d -> c p g d", g=G, p=P)
        out_c = out[0:TOKENS, :].rearrange("(c g p) d -> c p g d", g=G, p=P)
        slots_e = slots.rearrange("(e j p) r -> e p j r", e=EXPERTS, p=P)

        def norms_of(s):
            return slice(0 if s.back(-1).valid() else 1, 2 if s.back(2).valid() else 1)

        def head_start(engine, *sems):
            for s in sems:
                engine.sem_inc(s, HEAD)

        def group_head_start(engine, *sems):
            for s in sems:
                engine.sem_inc(s, GROUP_HEAD)

        block = stack.enter_context(nc.Block())

        @block.sync
        def _(sp):
            def load(c):
                if not c.valid():
                    return
                if not (c.known and c.number < RING):
                    sp.wait_ge(x1_made, done(c.back(RING)))
                    sp.wait_ge(kv_projected, done(c.back(RING)))
                if c.known:
                    x_src, ct_src = x_c[c.number], ctx_t[:, c.number * TOK:(c.number + 1) * TOK]
                else:
                    x_src = x_c[bass.ds(c.number, 1)].rearrange("c p g d -> (c p) g d")
                    ct_src = ctx_t[:, bass.ds(c.number * TOK, TOK)]
                sp.dma_start(ct_sb[:, c.k, :], ct_src).then_inc(ct_loaded[c.k], 16)
                sp.dma_start(x_sb[:, c.k], x_src).then_inc(x_loaded[c.k], 16)

            def store(c):
                if not c.valid():
                    return
                sp.wait_ge(x1_made, done(c))
                dst = out_c[c.number] if c.known else \
                    out_c[bass.ds(c.number, 1)].rearrange("c p g d -> (c p) g d")
                sp.dma_start(dst, x1[:, c.k % 2]).then_inc(x1_stored[c.k % 2], 16)

            def fill(c):
                if not c.valid():
                    return
                if not (c.known and c.number < RING):
                    sp.wait_ge(rows_sent[c.k], (c.it + 1) * (G * TOP_K * 16))
                    sp.sem_inc(waits_apart, 1)
                sp.wait_ge(rows_normed, done(c))
                sp.dma_start(rows[:, c.k, :, 0:D], xn2[:, c.k]).then_inc(rows_filled[c.k], 16)

            def step(s):
                load(s.back(-2))
                store(s.back(1))
                if s.k % 2 == 0:
                    fill(s.back(4))
                    fill(s.back(3))
                if s.known and s.number == 0:
                    sp.wait_ge(consts_made, 2)
                    sp.dma_start(out[TOKENS:TOKENS + P, :], empty_row[:, 0:D]).then_inc(dummies_stored, 16)
                    for par in range(2):
                        load_weights(0, par)

            def load_weights(i, par):
                e = i * 2 + par
                if isinstance(e, int):
                    up, down = w_in[e], w_out[e]
                else:
                    up = w_in[bass.ds(e, 1)].rearrange("e h i -> (e h) i")
                    down = w_out[bass.ds(e, 1)].rearrange("e i h -> (e i) h")
                sp.dma_start(wi_sb[:, par, :], up).then_inc(weights_loaded[par], 16)
                sp.dma_start(wo_sb[:, par, :].rearrange("p (t h) -> p t h", t=IT),
                             down.rearrange("(t p) h -> p t h", p=P)).then_inc(weights_loaded[par], 16)

            def load_slots(i, par):
                e = i * 2 + par
                src = slots_e[e] if isinstance(e, int) else \
                    slots_e[bass.ds(e, 1)].rearrange("e p j r -> (e p) j r")
                sp.dma_start(xg[:, par, 0:PAIR, :], src[:, 0:PAIR, :]).then_inc(xg_begun[par], 16)
                sp.dma_start(xg[:, par, PAIR:SLOT_TILES, :], src[:, PAIR:SLOT_TILES, :]).then_inc(xg_loaded[par], 16)

            for b in range(RING):
                sp.sem_inc(rows_filled[b], 16)
            sp.dma_start(bkv_sb[:, :], bkv.rearrange("(a d) -> a d", a=1).broadcast_to([P, 2 * D])) \
                .then_inc(kv_consts_loaded, 16)
            sp.dma_start(wkv_sb[:, :], wkv_t).then_inc(kv_consts_loaded, 16)
            load(Chunk(0, 0))
            sp.dma_start(wq_sb[:, :], wq_t).then_inc(small_loaded, 16)
            sp.dma_start(bq_sb[:, :], bq.rearrange("(p a) -> p a", a=1)).then_inc(small_loaded, 16)
            sp.dma_start(wr_sb[:, :], wr_t).then_inc(small_loaded, 16)
            sp.dma_start(br_sb[:, :], br.rearrange("(a d) -> a d", a=1).broadcast_to([P, EXPERTS])) \
                .then_inc(small_loaded, 16)
            steps(sp, step)
            sp.wait_ge(slots_ready, 1)
            load_slots(0, 0)
            sp.wait_ge(xg_loaded[0], 16)
            load_slots(0, 1)
            with sp.Fori(1, EXPERTS // 2) as i:
                for par in range(2):
                    sp.wait_ge(weights_low, i * 4 + (2 * par - 2))
                    load_weights(i, par)
                    sp.wait_ge(group_turned, group_done(Group(i - 1, par * GROUPS + GROUPS - 1)))
                    load_slots(i, par)

        @block.gpsimd
        def _(pool):
            order = Local(pool, pool_order)
            order.add(pool.memset(empty_row[:, :], 0.0))
            order.add(pool.memset(ident[:, :], 0.0))
            order.add(pool.memset(head_mask[:, :], 1.0))
            order.add(pool.memset(before[:, :], 1.0))
            pool.memset(ones[:, :], 1.0)
            pool.memset(eps_sb[:, :], LN_EPS)
            order.wait()
            order.add(pool.affine_select(out=ident[:, :], in_=ident[:, :], compare_op=ALU.not_equal, fill=1.0,
                                         base=0, pattern=[[-1, P]], channel_multiplier=1))
            order.add(pool.affine_select(out=head_mask[:, :], in_=head_mask[:, :], compare_op=ALU.is_ge, fill=0.0,
                                         base=0, pattern=[[-HD, HEADS], [0, HD]], channel_multiplier=1))
            order.wait()
            pool.affine_select(out=head_mask[:, :], in_=head_mask[:, :], compare_op=ALU.is_ge, fill=0.0,
                               base=HD - 1, pattern=[[HD, HEADS], [0, HD]], channel_multiplier=-1)
            pool.affine_select(out=before[:, :], in_=before[:, :], compare_op=ALU.is_gt, fill=0.0,
                               base=0, pattern=[[1, P]], channel_multiplier=-1)
            pool.iota(iota8[:, :], pattern=[[1, EXPERTS]], base=0, channel_multiplier=0,
                      allow_small_or_imprecise_dtypes=True)
            pool.iota(slot_base[:, :], pattern=[[CAPACITY, EXPERTS]], base=-int(NO_SLOT), channel_multiplier=0,
                      allow_small_or_imprecise_dtypes=True)
            pool.iota(token_no[:, :], pattern=[[P, TILES]], base=0, channel_multiplier=1)
            order.add(pool.iota(empty_row[:, ROW_TOKEN:ROW].bitcast(I32), pattern=[[0, 1]], base=TOKENS,
                                channel_multiplier=1))
            order.wait()
            pool.drain().then_inc(consts_made, 2)
            pool.sem_inc(experts_added, 2)
            per = EXPERTS // RING
            for e in range(EXPERTS):
                pool.dma_start(slots_e[e], empty_row[:, None, :].broadcast_to([P, SLOT_TILES, ROW])) \
                    .then_inc(rows_sent[e // per], G * TOP_K * 16 // per)

            def scatter(s, first_only=False):
                for j in range(DUO * TOP_K):
                    c = s.back(5 - j // (G * TOP_K))
                    if first_only and j % (G * TOP_K):
                        continue
                    pool.indirect_dma_start(
                        slots[:, :], bass.IndirectOffsetOnAxis(
                            ap=place_no[:, c.k // 2, j:j + 1], axis=0),
                        rows[:, c.k, j // TOP_K % G, :], None, bounds_check=SLOTS - 1, oob_is_err=False,
                    ).then_inc(rows_sent[c.k], 16 * G * TOP_K if first_only else 16)

            def step(s):
                if s.k % 2 == 0 or not s.back(4).valid():
                    return
                if s.known and s.number == CHUNKS + 3:
                    last_step(s)
                    return
                pool.wait_ge(place_ready, duo_done(s.back(5)))
                for h in (5, 4):
                    pool.wait_ge(rows_filled[s.back(h).k], s.back(h).it * 16 + 32)
                pool.sem_inc(waits_apart, 1)
                if not may_be_full(s.back(5)):
                    scatter(s)
                else:
                    last_use = s.back(5).number >= CHUNKS - RING
                    least = pool.value_load(fewest[0:1, s.back(5).number // 2:s.back(5).number // 2 + 1])
                    with pool.If(least < CAPACITY):
                        scatter(s)
                        if last_use:
                            landed(s)
                    if not last_use:
                        with pool.Else():
                            scatter(s, first_only=True)

            def landed(s):
                for h in (5, 4):
                    pool.wait_ge(rows_sent[s.back(h).k], G * TOP_K * 16 * (CHUNKS // RING + 1))

            def last_step(s):
                for b in range(RING):
                    pool.wait_ge(rows_sent[b], G * TOP_K * 16 * (CHUNKS // RING))
                pool.wait_ge(last_counted, 1)
                pool.sem_inc(waits_apart, 1)
                least = pool.value_load(fewest[0:1, s.back(5).number // 2:s.back(5).number // 2 + 1])
                with pool.If(least < CAPACITY):
                    pool.wait_ge(place_ready, duo_done(s.back(5)))
                    for h in (5, 4):
                        pool.wait_ge(rows_filled[s.back(h).k], s.back(h).it * 16 + 32)
                    pool.sem_inc(waits_apart, 1)
                    scatter(s)
                    landed(s)
                    pool.sem_inc(slots_ready, 1)
                with pool.Else():
                    pool.sem_inc(slots_ready, 1)

            for b in range(RING):
                pool.wait_ge(rows_sent[b], G * TOP_K * 16)
            steps(pool, step)

            for b in range(2):
                pool.wait_ge(x1_stored[b], 16 * (CHUNKS // 2))
            pool.wait_ge(dummies_stored, 16)
            with pool.Fori(0, EXPERTS // 2) as i:
                for par in range(2):
                    e = i * 2 + par
                    pool.wait_ge(gates_made, e + 1)
                    for g in range(GROUPS):
                        pool.wait_ge(y_made, group_done(Group(i, par * GROUPS + g)))
                        pool.sem_inc(waits_apart, 1)
                        for t in range(PAIR):
                            j = g * PAIR + t
                            pool.indirect_dma_start(
                                out[:, :], bass.IndirectOffsetOnAxis(
                                    ap=token[:, par, j:j + 1], axis=0),
                                y_sb[:, par, j, :], None, compute_op=ALU.add,
                            ).then_inc(rows_added, 16)
                    pool.wait_ge(rows_added, e * (16 * SLOT_TILES) + 16 * SLOT_TILES)
                    pool.sem_inc(experts_added, 1)

        @block.scalar
        def _(act):
            head_start(act, std_ready, x_normed, xnt_made, qt_made, v_made, kv_squared, kv_rooted, rows_normed,
                       x2t_made, exp_ready)
            act.wait_ge(consts_made, 2)
            act.activation(unused[:, :], eps_sb[:, :], ACT.Sqrt)

            def roots(s):
                n, l = s.back(-1), s.back(2)
                if n.valid() or l.valid():
                    act.wait_ge(var_ready, done(n))
                    if not (s.known and s.number < 0):
                        act.wait_ge(scales_ready, done(s))
                    act.activation(std[:, norms_of(s), :], mean_var[:, s.k % 2, norms_of(s), :, 1], ACT.Sqrt,
                                   bias=eps_sb[:, :]).then_inc(std_ready, 1)

            def norm1(c):
                if not c.valid():
                    return
                act.wait_ge(scales_ready, done(c))
                if not (c.known and c.number < 2):
                    act.wait_ge(x_turned, done(c.back(2)))
                for g in range(G):
                    ins = act.activation(xn[:, c.k % 2, g, :], x_sb[:, c.k, g, :], ACT.Identity,
                                         scale=scales[:, 1 - c.k % 2, 0, 0, g:g + 1], bias=scales[:, 1 - c.k % 2, 1, 0, g:g + 1])
                ins.then_inc(x_normed, 1)

            def high_part(i, par, which):
                act.wait_ge(weights_loaded[par], i * 32 + 32)
                act.copy((wi_hi, wo_hi)[which][:, par, :], (wi_sb, wo_sb)[which][:, par, :]).then_inc(weights_high, 1)

            def step(s):
                n, l = s.back(-1), s.back(2)
                if s.known and s.number == 0:
                    act.wait_ge(small_loaded, 16 * 4)
                if s.known and s.number == CHUNKS + 1:
                    for which in range(2):
                        high_part(0, 0, which)
                if s.valid():
                    act.wait_ge(kv_projected, done(s))
                    if not (s.known and s.number < 1):
                        act.wait_ge(norms_ready, done(s.back(1)))
                    act.activation(sq[:, :, :, :], ps_kv, ACT.Square).then_inc(kv_squared, 1)
                roots(s)
                if s.valid():
                    act.wait_ge(x_turned, done(s))
                    if not (s.known and s.number < 1):
                        act.wait_ge(q_projected, done(s.back(1)))
                    act.copy(xnt[:, :], ps_t).then_inc(xnt_made, 1)
                if s.valid():
                    if not (s.known and s.number < 2):
                        act.wait_ge(state_summed, done(s.back(2)))
                    act.copy(kvb[:, s.k % 2, :, 1, :], ps_kv[:, :, 1, :]).then_inc(v_made, 1)
                if l.valid():
                    act.wait_ge(scales_ready, done(n))
                    if not (l.known and l.number < RING):
                        act.wait_ge(rows_filled[l.k], l.it * 16 + 16)
                    for g in range(G):
                        ins = act.activation(xn2[:, l.k, g, :], x1[:, l.k % 2, g, :], ACT.Identity,
                                             scale=scales[:, s.k % 2, 0, 1, g:g + 1], bias=scales[:, s.k % 2, 1, 1, g:g + 1])
                    ins.then_inc(rows_normed, 1)
                if s.valid():
                    act.wait_ge(norms_ready, done(s))
                    act.activation(kv_norm[:, :, :, :], ss[:, :, :, :], ACT.Sqrt).then_inc(kv_rooted, 1)
                if s.k % 2 == 0 and s.back(4).valid():
                    act.wait_ge(shift_ready, duo_done(s.back(4)))
                    act.activation(expo[:, :, :], shifted[:, :, :], ACT.Exp).then_inc(exp_ready, 1)
                if s.valid():
                    act.wait_ge(q_projected, done(s))
                    if not (s.known and s.number < 2):
                        act.wait_ge(attended, done(s.back(2)))
                    act.activation(qt[:, s.k % 2, :], ps_q, ACT.Identity, bias=bq_sb[:, :]).then_inc(qt_made, 1)
                if l.valid():
                    act.wait_ge(rows_turned, done(l))
                    if not (l.known and l.number < 1):
                        act.wait_ge(logits_ready, done(l.back(1)))
                    act.copy(x2t[:, :], ps_t).then_inc(x2t_made, 1)
                norm1(n)
                if s.k % 2 == 0 and s.back(4).valid() and l.valid():
                    act.activation(unused[:, :], eps_sb[:, :], ACT.Sqrt)

            steps(act, step)
            group_head_start(act, xgt_high, hid_high, y_made, yt_made)

            def b_step(n):
                t, y = n.next(1), n.next(-2)
                if y.valid():
                    act.wait_ge(down_done, group_done(y))
                    act.wait_ge(y_turned, group_done(y.next(-2)))
                    act.copy(yt[:, y.b, :], ps3[:, 512 * y.b:512 * y.b + PG]).then_inc(yt_made, 1)
                if t.valid():
                    act.wait_ge(group_turned, group_done(t))
                    act.wait_ge(up_done, group_done(t.next(-2)))
                    act.copy(xgt_hi[:, t.b, :], ps2[:, 512 * t.b:512 * t.b + PG]).then_inc(xgt_high, 1)
                if n.valid():
                    act.wait_ge(up_done, group_done(n))
                    act.wait_ge(down_done, group_done(n.next(-2)))
                    act.activation(hid_hi[:, n.b, :], [ps0, ps1][n.b][:, :], ACT.Relu).then_inc(hid_high, 1)
                if y.valid():
                    if y.g == 0:
                        act.wait_ge(gates_made, y.expert + 1)
                        act.wait_ge(experts_added, y.expert + 1)
                    act.wait_ge(y_turned, group_done(y))
                    for q in range(PAIR):
                        j = y.g * PAIR + q
                        ins = act.activation(y_sb[:, y.par, j, :],
                                             ps3[:, 512 * y.b + PG + P * q:512 * y.b + PG + P * (q + 1)],
                                             ACT.Copy, scale=gate[:, y.par, j:j + 1])
                    ins.then_inc(y_made, 1)
                e = n.next(GROUPS)
                if n.valid() and n.g in (1, 2) and e.valid():
                    high_part(e.i, e.par, n.g - 1)

            group_steps(b_step)(act)

        @block.vector
        def _(dve):
            order = Local(dve, dve_order)
            head_start(dve, var_ready, scales_ready, norms_ready, kn_made, state_made, x1_made,
                       shift_ready, routed_ready, rank_read, place_ready)
            order.add(dve.memset(earlier[:, 0, :], 0.0))
            def spread(scalars):
                return scalars.broadcast_to([P, DUO, EXPERTS])

            def stats(n):
                dve.wait_ge(x_loaded[n.k], (n.it + 1) * 16)
                for g in range(G):
                    ins = dve.bn_stats(sums[:, 1 - n.k % 2, 0, g, :], x_sb[:, n.k, g, :])
                order.add(ins, "sums 1")

            def means(s):
                order.wait("sums 1" if s.back(-1).valid() else "sums 2", waits_apart)
                for ln in range(2)[norms_of(s)]:
                    for g in range(G):
                        ins = dve.bn_aggr(mean_var[:, s.k % 2, ln, g, :], sums[:, s.k % 2, ln, g, :])
                ins.then_inc(var_ready, 1)

            def invert(s):
                dve.wait_ge(std_ready, done(s.back(-1)))
                order.add(dve.reciprocal(scales[:, s.k % 2, 0, norms_of(s), :], std[:, norms_of(s), :]), "inverse")

            def shift(s):
                order.wait("inverse")
                dve.scalar_tensor_tensor(scales[:, s.k % 2, 1, norms_of(s), :], mean_var[:, s.k % 2, norms_of(s), :, 0], -1.0,
                                         scales[:, s.k % 2, 0, norms_of(s), :], ALU.mult, ALU.mult).then_inc(scales_ready, 1)

            def sum_squares(s):
                dve.wait_ge(kv_squared, done(s))
                order.add(dve.tensor_reduce(ss[:, :, :, :], sq[:, :, :, :].rearrange("p g a (h i) -> p g a h i", i=HD),
                                            AX.X, ALU.add), "squares")

            def guard_norms(s):
                order.wait("squares")
                dve.tensor_scalar(ss[:, :, :, :], ss[:, :, :, :], L2_EPS * L2_EPS, None, ALU.max).then_inc(norms_ready, 1)

            def mask_state(a):
                dve.wait_ge(state_summed, done(a))
                if not (a.known and a.number < 1):
                    dve.wait_ge(attended, done(a.back(1)))
                dve.tensor_tensor(state[:, :, :, :].rearrange("p h g d -> p (h g) d"),
                                  ps_state.rearrange("p h g d -> p (h g) d"),
                                  head_mask[:, None, :].broadcast_to([P, 2 * G, D]),
                                  ALU.mult).then_inc(state_made, 1)

            def norm_products(s):
                dve.wait_ge(kv_rooted, done(s))
                order.add(dve.tensor_tensor(key_scale[:, :, :], kv_norm[:, :, 0, :], kv_norm[:, :, 1, :], ALU.mult), "norms")

            def invert_norms(s):
                order.wait("norms")
                order.add(dve.reciprocal(key_scale[:, :, :], key_scale[:, :, :]), "key scale")

            def scale_keys(s):
                if not (s.known and s.number < 2):
                    dve.wait_ge(state_summed, done(s.back(2)))
                dve.wait_ge(v_made, done(s))
                order.wait("key scale")
                dve.tensor_tensor(kvb[:, s.k % 2, :, 0, :].rearrange("p g (h i) -> p g h i", i=HD),
                                  ps_kv[:, :, 0, :].rearrange("p g (h i) -> p g h i", i=HD),
                                  key_scale[:, :, :, None].broadcast_to([P, G, HEADS, HD]),
                                  ALU.mult).then_inc(kn_made, 1)

            def residual(a):
                dve.wait_ge(attended, done(a))
                if not (a.known and a.number < 2):
                    dve.wait_ge(x1_stored[a.k % 2], (a.it * RING + a.k - a.k % 2) * 8)
                    dve.wait_ge(rows_normed, done(a.back(2)))
                dve.tensor_tensor(x1[:, a.k % 2], x_sb[:, a.k], ps_o, ALU.add).then_inc(x1_made, 1)

            def stats2(a):
                dve.wait_ge(x1_made, done(a))
                for g in range(G):
                    ins = dve.bn_stats(sums[:, a.k % 2, 1, g, :], x1[:, a.k % 2, g, :])
                order.add(ins, "sums 2")

            def even_step(s):
                n, a, l = s.back(-1), s.back(1), s.back(2)
                routing = s.back(4).valid()
                if n.valid():
                    stats(n)
                if s.known and s.number == CHUNKS + 2:
                    dve.wait_ge(last_summed, 1)
                    dve.tensor_reduce(fewest[0:1, s.back(4).number // 2:s.back(4).number // 2 + 1], ps_last[0:1, :],
                                      AX.X, ALU.min).then_inc(last_counted, 1)
                if n.valid() or l.valid():
                    means(s)
                if routing:
                    dve.wait_ge(logits_ready, done(s.back(3)))
                    order.add(dve.tensor_tensor(logit[:, :, :], ps_logit, spread(br_sb[:, None, :]), ALU.add), "logits")
                if routing:
                    order.wait("logits", waits_apart)
                    for g in range(DUO):
                        ins = dve.max(best[:, g, :], logit[:, g, :])
                    order.add(ins, "best")
                if n.valid() or l.valid():
                    invert(s)
                if routing:
                    order.wait("best")
                    dve.tensor_tensor(shifted[:, :, :], logit[:, :, :], spread(best[:, :, 0:1]),
                                      ALU.subtract).then_inc(shift_ready, 1)
                if n.valid() or l.valid():
                    shift(s)
                if s.valid():
                    sum_squares(s)
                if s.valid():
                    guard_norms(s)
                if routing:
                    for g in range(DUO):
                        ins = dve.max_index(best_no[:, g, :], best[:, g, :], logit[:, g, :])
                    order.add(ins, "best numbers")
                if a.valid():
                    mask_state(a)
                if routing:
                    order.wait("best numbers")
                    order.add(dve.tensor_tensor(
                        chosen[:, :, :, :], best_no[:, :, 0:TOP_K, None].broadcast_to([P, DUO, TOP_K, EXPERTS]),
                        iota8[:, None, None, :].broadcast_to([P, DUO, TOP_K, EXPERTS]), ALU.is_equal), "chosen")
                if s.valid():
                    norm_products(s)
                if routing:
                    order.wait("chosen")
                    order.add(dve.tensor_tensor(either[:, :, :], chosen[:, :, 0, :], chosen[:, :, 1, :], ALU.add), "either")
                if s.valid():
                    invert_norms(s)
                    scale_keys(s)
                if a.valid():
                    residual(a)
                if routing:
                    dve.wait_ge(exp_ready, duo_done(s.back(4)))
                    order.add(dve.tensor_reduce(total[:, :], expo[:, :, :], AX.X, ALU.add), "total")
                if a.valid():
                    stats2(a)
                if routing:
                    order.wait("total")
                    order.add(dve.reciprocal(total[:, :], total[:, :]), "inverse total")

            def odd_step(s):
                n, a, l, r = s.back(-1), s.back(1), s.back(2), s.back(5)
                routing = s.back(4).valid()
                if n.valid():
                    stats(n)
                if routing:
                    order.wait("inverse total")
                    order.add(dve.tensor_tensor(prob[:, :, :], expo[:, :, :], spread(total[:, :, None]), ALU.mult), "prob")
                if routing:
                    if not (r.known and r.number < RING):
                        for c in (r, s.back(4)):
                            dve.wait_ge(rows_sent[c.k], (c.it + 1) * (G * TOP_K * 16))
                    gates = rows[:, r.k:r.k + 2, :, ROW_GATE:ROW_TOKEN].rearrange("p k g e -> p (k g) e")
                    order.wait("prob")
                    order.add(dve.tensor_tensor(gates, prob[:, :, :], either[:, :, :], ALU.mult), "gates")
                if n.valid() or l.valid():
                    means(s)
                if routing:
                    order.wait("gates")
                    dve.tensor_scalar(routed[:, :, :], gates, 0.0, None, ALU.is_gt).then_inc(routed_ready, 1)
                if routing:
                    dve.wait_ge(routed_ready, duo_done(r))
                    order.add(dve.tensor_reduce(in_chunk[:, :], routed[:, :, :].rearrange("p g e -> p e g"),
                                                AX.X, ALU.add), "in chunk")
                if n.valid() or l.valid():
                    invert(s)
                if routing:
                    order.wait("in chunk")
                    duo = r.k // 2
                    order.add(dve.tensor_tensor(earlier[:, 1 - duo, :], earlier[:, duo, :], in_chunk[:, :], ALU.add))
                if n.valid() or l.valid():
                    shift(s)
                if s.valid():
                    sum_squares(s)
                if routing:
                    tiles = token_no[:, r.number * G:r.number * G + DUO] if r.known else \
                        token_no[:, bass.ds(r.number * G, DUO)]
                    dve.tensor_copy(rows[:, r.k:r.k + 2, :, ROW_TOKEN].rearrange("p k g -> p (k g)").bitcast(I32), tiles)
                if s.valid():
                    guard_norms(s)
                if a.valid():
                    mask_state(a)
                if routing:
                    dve.wait_ge(rank_ready, duo_done(r))
                    order.add(dve.scalar_tensor_tensor(fits[:, :, :], ps_rank, float(CAPACITY), routed[:, :, :],
                                                       ALU.is_lt, ALU.mult))
                    order.add(dve.tensor_tensor(place[:, :, :], ps_rank, spread(slot_base[:, None, :]), ALU.add), "places")
                    if may_be_full(r) and s.number < CHUNKS + 3:
                        dve.tensor_reduce(fewest[0:1, r.number // 2:r.number // 2 + 1], ps_rank[0:1, 0, :], AX.X, ALU.min)
                if s.valid():
                    norm_products(s)
                if routing:
                    order.wait("places")
                    dve.tensor_tensor(place[:, :, :], place[:, :, :], fits[:, :, :], ALU.mult).then_inc(rank_read, 1)
                if s.valid():
                    invert_norms(s)
                if routing:
                    dve.wait_ge(rank_read, duo_done(r))
                    order.add(dve.tensor_tensor(
                        place_k[:, :, :, :], chosen[:, :, :, :],
                        place[:, :, None, :].broadcast_to([P, DUO, TOP_K, EXPERTS]), ALU.mult), "places by choice")
                if s.valid():
                    scale_keys(s)
                if routing:
                    order.wait("places by choice")
                    order.add(dve.tensor_reduce(place_f[:, :, :], place_k[:, :, :, :], AX.X, ALU.add), "slots")
                if a.valid():
                    residual(a)
                if routing:
                    order.wait("slots")
                    dve.tensor_scalar(place_no[:, r.k // 2, :], place_f[:, :, :].rearrange("p g k -> p (g k)"),
                                      NO_SLOT, None, ALU.add).then_inc(place_ready, 1)
                if a.valid():
                    stats2(a)

            def split_biases():
                dve.wait_ge(consts_made, 2)
                dve.wait_ge(kv_consts_loaded, 16 * 2)
                left = bkv_sb
                for r in range(3):
                    order.add(dve.tensor_copy(bkv_part[:, r, :], left[:, :]))
                    order.wait()
                    if r == 0:
                        order.add(dve.tensor_scalar(bkv_rows[:, :], bkv_part[:, r, :], ident[:, r:r + 1], None, ALU.mult))
                    else:
                        order.add(dve.scalar_tensor_tensor(bkv_rows[:, :], bkv_part[:, r, :], ident[:, r:r + 1],
                                                           bkv_rows[:, :], ALU.mult, ALU.add))
                    if r < 2:
                        order.add(dve.tensor_tensor(bkv_rest[:, :], left[:, :], bkv_part[:, r, :], ALU.subtract))
                        order.wait()
                        left = bkv_rest
                order.wait()
                dve.sem_inc(bias_ready, 1)

            def low_part(e, par, which):
                hi, raw, lo = (wi_hi, wi_sb, wi_lo) if which == 0 else (wo_hi, wo_sb, wo_lo)
                dve.wait_ge(weights_high, e * 2 + (1 + which))
                dve.tensor_tensor(lo[:, par, :], raw[:, par, :], hi[:, par, :].bitcast(F32),
                                  ALU.subtract).then_inc(weights_low, 1)

            def step(s):
                if s.known and s.number == -1:
                    split_biases()
                if s.known and s.number == 0:
                    dve.wait_ge(small_loaded, 16 * 4)
                if s.k % 2 == 0:
                    even_step(s)
                else:
                    odd_step(s)
                if s.known and s.number == CHUNKS + 1:
                    for which in range(2):
                        low_part(0, 0, which)

            steps(dve, step, order, DVE_PER_TURN)

            group_head_start(dve, xgt_low, hid_low)

            def b_step(n):
                t = n.next(1)
                if t.valid():
                    dve.wait_ge(xgt_high, group_done(t))
                    dve.tensor_tensor(xgt_lo[:, t.b, :], ps2[:, 512 * t.b:512 * t.b + PG],
                                      xgt_hi[:, t.b, :].bitcast(F32), ALU.subtract).then_inc(xgt_low, 1)
                    if t.g == 1:
                        dve.wait_ge(xg_loaded[t.par], t.i * 16 + 16)
                        column = ROW_GATE + t.expert
                        src = xg[:, t.par, :, column] if isinstance(column, int) else \
                            xg[:, t.par, :, bass.ds(column, 1)].rearrange("p j a -> p (j a)")
                        dve.tensor_copy(gate[:, t.par, :], src)
                        dve.wait_ge(experts_added, t.expert + 1)
                        dve.tensor_copy(token[:, t.par, :], xg[:, t.par, :, ROW_TOKEN].bitcast(I32)).then_inc(gates_made, 1)
                if n.valid():
                    dve.wait_ge(hid_high, group_done(n))
                    dve.wait_ge(down_done, group_done(n.next(-2)))
                    dve.scalar_tensor_tensor(hid_lo[:, n.b, :], [ps0, ps1][n.b][:, :], 0.0,
                                             hid_hi[:, n.b, :].bitcast(F32), ALU.max,
                                             ALU.subtract).then_inc(hid_low, 1)
                e = n.next(GROUPS)
                if n.valid() and n.g in (1, 2) and e.valid():
                    low_part(e.expert, e.par, n.g - 1)

            group_steps(b_step)(dve)

        @block.tensor
        def _(pe):
            head_start(pe, x_turned, kv_projected, q_projected, state_summed, attended, rows_turned, logits_ready,
                       rank_ready)
            pe.wait_ge(consts_made, 2)

            def step(s):
                n, a, l = s.back(-1), s.back(1), s.back(2)
                if a.valid():
                    pe.wait_ge(kn_made, done(a))
                    pe.wait_ge(v_made, done(a))
                    if not (a.known and a.number < 1):
                        pe.wait_ge(state_made, done(a.back(1)))
                    for g in range(G):
                        for h in range(2):
                            half = slice(SEQ * h, SEQ * (h + 1))
                            ins = pe.matmul(ps_state[:, h, g, :], kvb[half, a.k % 2, g, 0, :], kvb[half, a.k % 2, g, 1, :],
                                            start=True, stop=True)
                    ins.then_inc(state_summed, 1)
                if s.k % 2 == 1 and s.back(4).valid():
                    r = s.back(5)
                    pe.wait_ge(routed_ready, duo_done(r))
                    pe.matmul(ps_rank, before[:, :], routed[:, :, :], start=True, stop=False)
                    for g in range(1, DUO):
                        pe.matmul(ps_rank[:, g:DUO, :], ones[:, :], routed[:, 0:DUO - g, :], start=False, stop=False)
                    pe.matmul(ps_rank, ones[:, :], earlier[:, r.k // 2, None, :].broadcast_to([P, DUO, EXPERTS]),
                              start=False, stop=True).then_inc(rank_ready, 1)
                if s.known and s.number == 0:
                    pe.wait_ge(small_loaded, 16 * 4)
                if s.valid():
                    pe.wait_ge(xnt_made, done(s))
                    if not (s.known and s.number < 1):
                        pe.wait_ge(qt_made, done(s.back(1)))
                    pe.matmul(ps_q, wq_sb[:, :], xnt[:, :], start=True, stop=True).then_inc(q_projected, 1)
                if l.valid():
                    pe.wait_ge(rows_normed, done(l))
                    if not (s.known and not s.valid()):
                        pe.wait_ge(xnt_made, done(s))
                    for g in range(G):
                        ins = pe.transpose(ps_t[:, P * g:P * (g + 1)], xn2[:, l.k, g, :], ident[:, :])
                    ins.then_inc(rows_turned, 1)
                if a.valid():
                    pe.wait_ge(qt_made, done(a))
                    pe.wait_ge(state_made, done(a))
                    if not (a.known and a.number < 1):
                        pe.wait_ge(x1_made, done(a.back(1)))
                    for g in range(G):
                        for h in range(2):
                            tokens = slice(P * g + SEQ * h, P * g + SEQ * (h + 1))
                            ins = pe.matmul(ps_o[SEQ * h:SEQ * (h + 1), g, :], qt[:, a.k % 2, tokens], state[:, h, g, :],
                                            start=True, stop=True)
                    ins.then_inc(attended, 1)
                if s.known and s.number == -1:
                    pe.wait_ge(kv_consts_loaded, 16 * 2)
                    pe.wait_ge(bias_ready, 1)
                if n.valid():
                    pe.wait_ge(ct_loaded[n.k], (n.it + 1) * 16)
                    if not (n.known and n.number < 1):
                        pe.wait_ge(kn_made, done(s))
                        pe.wait_ge(v_made, done(s))
                    for g in range(G):
                        bank = ps0[:, 256 * g:256 * (g + 1)]
                        pe.matmul(bank, ct_sb[:, n.k, P * g:P * (g + 1)], wkv_sb[:, :], start=True, stop=False)
                        ins = pe.matmul(bank, ones[:, :], bkv_rows[:, :], start=False, stop=True)
                    ins.then_inc(kv_projected, 1)
                if l.valid():
                    pe.wait_ge(x2t_made, done(l))
                    if s.k % 2 == 0 and s.back(4).valid():
                        pe.wait_ge(shift_ready, duo_done(s.back(4)))
                    if s.k % 2 == 1 and s.back(4).valid():
                        pe.wait_ge(rank_read, duo_done(s.back(5)))
                    for g in range(G):
                        ins = pe.matmul(ps_logit[:, l.k % 2 * G + g, :], x2t[:, P * g:P * (g + 1)], wr_sb[:, :],
                                        start=True, stop=True)
                    ins.then_inc(logits_ready, 1)
                if s.known and s.number == CHUNKS + 1:
                    pe.wait_ge(rank_read, duo_done(s.back(5)))
                    pe.matmul(ps_last, ones[:, :], earlier[:, 1 - s.back(5).k // 2, :],
                              start=True, stop=True).then_inc(last_summed, 1)
                if n.valid():
                    pe.wait_ge(x_normed, done(n))
                    if l.valid():
                        pe.wait_ge(x2t_made, done(l))
                    elif s.valid():
                        pe.wait_ge(xnt_made, done(s))
                    for g in range(G):
                        ins = pe.transpose(ps_t[:, P * g:P * (g + 1)], xn[:, n.k % 2, g, :], ident[:, :])
                    ins.then_inc(x_turned, 1)

            steps(pe, step)

            group_head_start(pe, group_turned, up_done, down_done, y_turned)

            def b_step(n):
                t, m, y = n.next(1), n.next(-1), n.next(-2)
                if t.valid():
                    if t.g < 2:
                        pe.wait_ge((xg_begun, xg_loaded)[t.g][t.par], t.i * 16 + 16)
                    pe.wait_ge(xgt_low, group_done(t.next(-2)))
                    for q in range(PAIR):
                        ins = pe.transpose(ps2[:, 512 * t.b + P * q:512 * t.b + P * (q + 1)],
                                           xg[:, t.par, t.g * PAIR + q, 0:D], ident[:, :])
                    ins.then_inc(group_turned, 1)
                if n.valid():
                    if n.g == 0:
                        pe.wait_ge(weights_low, n.expert * 2 + 2)
                    pe.wait_ge(xgt_low, group_done(n))
                    pe.wait_ge(hid_low, group_done(n.next(-2)))
                    for t in range(IT):
                        bank = [ps0, ps1][n.b][:, PG * t:PG * (t + 1)]
                        w_hi, w_lo = (w[:, n.par, P * t:P * (t + 1)] for w in (wi_hi, wi_lo))
                        pe.matmul(bank, w_hi, xgt_hi[:, n.b, :], start=True, stop=False)
                        pe.matmul(bank, w_hi, xgt_lo[:, n.b, :], start=False, stop=False)
                        ins = pe.matmul(bank, w_lo, xgt_hi[:, n.b, :], start=False, stop=True)
                    ins.then_inc(up_done, 1)
                if y.valid():
                    pe.wait_ge(yt_made, group_done(y))
                    pe.wait_ge(y_made, group_done(y.next(-2)))
                    for q in range(PAIR):
                        ins = pe.transpose(ps3[:, 512 * y.b + PG + P * q:512 * y.b + PG + P * (q + 1)],
                                           yt[:, y.b, P * q:P * (q + 1)], ident[:, :])
                    ins.then_inc(y_turned, 1)
                if m.valid():
                    pe.wait_ge(hid_low, group_done(m))
                    pe.wait_ge(y_made, group_done(m.next(-2)))
                    bank = ps3[:, 512 * m.b:512 * m.b + PG]
                    for t in range(IT):
                        h_hi, h_lo = (h[:, m.b, PG * t:PG * (t + 1)] for h in (hid_hi, hid_lo))
                        w_hi, w_lo = (w[:, m.par, D * t:D * (t + 1)] for w in (wo_hi, wo_lo))
                        pe.matmul(bank, w_hi, h_hi, start=(t == 0), stop=False)
                        pe.matmul(bank, w_hi, h_lo, start=False, stop=False)
                        ins = pe.matmul(bank, w_lo, h_hi, start=False, stop=(t == IT - 1))
                    ins.then_inc(down_done, 1)

            group_steps(b_step)(pe)


def kernel(x, ctx_1024, L0_xattn_Wq, L0_xattn_bq, L0_xattn_Wk, L0_xattn_bk, L0_xattn_Wv, L0_xattn_bv,
           L0_ffn_W_router, L0_ffn_b_router, L0_ffn_experts_inter, L0_ffn_experts_out):
    import numpy as np
    import concourse.bacc as bacc
    from concourse.bass_utils import run_bass_kernel_spmd

    nc = bacc.Bacc("TRN2", target_bir_lowering=False, num_devices=1)
    arrays = {
        "x": np.asarray(x).reshape(TOKENS, D),
        "ctx_t": np.asarray(ctx_1024).reshape(TOKENS, D).T,
        "wq_t": np.asarray(L0_xattn_Wq).T,
        "bq": np.asarray(L0_xattn_bq),
        "wkv_t": np.concatenate([np.asarray(L0_xattn_Wk).T, np.asarray(L0_xattn_Wv).T], axis=1),
        "bkv": np.concatenate([np.asarray(L0_xattn_bk), np.asarray(L0_xattn_bv)]),
        "wr_t": np.asarray(L0_ffn_W_router).T,
        "br": np.asarray(L0_ffn_b_router),
        "w_in": np.asarray(L0_ffn_experts_inter),
        "w_out": np.asarray(L0_ffn_experts_out),
    }
    arrays = {name: np.ascontiguousarray(a) for name, a in arrays.items()}
    drams = [nc.dram_tensor(name + "_dram", a.shape, F32, kind="ExternalInput").ap() for name, a in arrays.items()]
    out = nc.dram_tensor("out_dram", (TOKENS + P, D), F32, kind="ExternalOutput").ap()
    slots = nc.dram_tensor("slots_dram", (SLOTS, ROW), F32).ap()
    build(nc, *drams, out, slots)
    r = run_bass_kernel_spmd(nc, [{name + "_dram": a for name, a in arrays.items()}], core_ids=[0])
    return r.results[0]["out_dram"][0:TOKENS].reshape(BATCHES, SEQ, D)
```
